# Optimizing a Trainium2 kernel written in Bass

```python
import numpy as np
import jax
import jax.numpy as jnp

def _softmax(x, axis=-1):
    return jax.nn.softmax(x, axis=axis)

def _gelu(x):
    return jax.nn.gelu(x, approximate=True)

def _silu(x):
    return jax.nn.silu(x)

def _sigmoid(x):
    return jax.nn.sigmoid(x)

def _layernorm(x, axis=-1, eps=1e-05):
    m = jnp.mean(x, axis=axis, keepdims=True)
    v = jnp.var(x, axis=axis, keepdims=True)
    return (x - m) / jnp.sqrt(v + eps)

def _scatter_add(tgt, idx, src, axis=0):
    return tgt.at[idx].add(src)

def _segment_sum(src, seg, n):
    return jax.ops.segment_sum(src, seg, n)
kernel_name = 'mk_audio_tower_d1_tok_audfeat256_r4_0cbbad'

def setup_inputs(seed: int=0):
    np.random.seed(seed)
    _w = jnp.asarray

    def _rec_inputs():
        import jax
        import jax.numpy as jnp
        _rk = jax.random.key(seed)
        x = -0.00197248 + 1.00072 * jax.random.normal(jax.random.fold_in(_rk, 1), (64, 1, 10240), jnp.float32)
        return x
    x = _rec_inputs()

    def _L0_tok_setup():
        import jax, jax.numpy as jnp
        import numpy as np
        B, L = (4, 10240)
        C = 128
        DMLP = 512
        TEMP = 1e-05
        EPS = 1e-05
        FACTOR = 2

        def _conv(x, w, b, stride, pad):
            x = jnp.pad(x, ((0, 0), (0, 0), (pad, pad)), mode='reflect')
            y = jax.lax.conv_general_dilated(x, w, (stride,), 'VALID', dimension_numbers=('NCH', 'OIH', 'NCH'))
            return y + b[None, :, None]

        def _cnorm(x, g, b):
            m = jnp.mean(x, axis=1, keepdims=True)
            v = jnp.var(x, axis=1, keepdims=True, ddof=1)
            return (x - m) * jax.lax.rsqrt(v + EPS) * g[None, :, None] + b[None, :, None]

        def _forward(x, conv0_w, conv0_b, conv1_w, conv1_b, conv2_w, conv2_b, conv3_w, conv3_b, n0_w, n0_b, n1_w, n1_b, n2_w, n2_b, n3_w, n3_b, n4_w, n4_b, mlp_w1, mlp_b1, mlp_w2, mlp_b2, mlp_w3, mlp_b3):
            h = jax.nn.relu(_cnorm(_conv(x, conv0_w, conv0_b, 5, 3), n0_w, n0_b))
            h = jax.nn.relu(_cnorm(_conv(h, conv1_w, conv1_b, 4, 2), n1_w, n1_b))
            h = jax.nn.relu(_cnorm(_conv(h, conv2_w, conv2_b, 2, 1), n2_w, n2_b))
            h = jax.nn.relu(_cnorm(_conv(h, conv3_w, conv3_b, 2, 1), n3_w, n3_b))
            f = jnp.transpose(h, (0, 2, 1))
            T = f.shape[1]
            z = jax.nn.gelu(f @ mlp_w1 + mlp_b1, approximate=False)
            z = jax.nn.gelu(z @ mlp_w2 + mlp_b2, approximate=False)
            imp = jax.nn.sigmoid((z @ mlp_w3 + mlp_b3)[..., 0]) + TEMP
            imp = imp / jnp.sum(imp, axis=1, keepdims=True) * (T / FACTOR)
            Tn = T // FACTOR
            cs = jnp.cumsum(imp, axis=1)
            p = jnp.maximum(cs[:, :, None] - jnp.arange(Tn, dtype=cs.dtype)[None, None, :], 0.0)
            pc = jnp.pad(p, ((0, 0), (0, 0), (0, 1)))
            d = pc[:, :, :-1] - pc[:, :, 1:]
            wmat = d - jnp.pad(d, ((0, 0), (1, 0), (0, 0)))[:, :-1, :]
            pooled = jnp.einsum('btn,btc->bnc', wmat, f)
            out = jnp.transpose(pooled, (0, 2, 1))
            return jax.nn.relu(_cnorm(out, n4_w, n4_b))
        key = jax.random.key(seed)
        ks = jax.random.split(key, 8)

        def w(k, shape, fan_in):
            return jax.random.normal(k, shape, jnp.float32) / np.float32(np.sqrt(fan_in))
        inp = {'x': jax.random.normal(ks[0], (B, 1, L), jnp.float32), 'conv0_w': w(ks[1], (C, 1, 10), 10), 'conv0_b': jnp.zeros(C, jnp.float32), 'conv1_w': w(ks[2], (C, C, 8), C * 8), 'conv1_b': jnp.zeros(C, jnp.float32), 'conv2_w': w(ks[3], (C, C, 4), C * 4), 'conv2_b': jnp.zeros(C, jnp.float32), 'conv3_w': w(ks[4], (C, C, 4), C * 4), 'conv3_b': jnp.zeros(C, jnp.float32), 'mlp_w1': w(ks[5], (C, DMLP), C), 'mlp_b1': jnp.zeros(DMLP, jnp.float32), 'mlp_w2': w(ks[6], (DMLP, DMLP), DMLP), 'mlp_b2': jnp.zeros(DMLP, jnp.float32), 'mlp_w3': w(ks[7], (DMLP, 1), DMLP), 'mlp_b3': jnp.zeros(1, jnp.float32)}
        for i in range(5):
            inp[f'n{i}_w'] = jnp.ones(C, jnp.float32)
            inp[f'n{i}_b'] = jnp.zeros(C, jnp.float32)
        return inp
    _L0_tok_all = _L0_tok_setup()
    _L0_tok_in = {k: v for k, v in _L0_tok_all.items() if k in ('conv0_w', 'conv0_b', 'conv1_w', 'conv1_b', 'conv2_w', 'conv2_b', 'conv3_w', 'conv3_b', 'n0_w', 'n0_b', 'n1_w', 'n1_b', 'n2_w', 'n2_b', 'n3_w', 'n3_b', 'n4_w', 'n4_b', 'mlp_w1', 'mlp_b1', 'mlp_w2', 'mlp_b2', 'mlp_w3', 'mlp_b3')}
    del _L0_tok_all

    def _L0_attn_setup():
        import jax, jax.numpy as jnp
        import numpy as np
        import math
        B, T, D_MODEL = (1, 512, 64)
        N_Q, N_KV = (16, 1)
        D_HEAD = D_MODEL // N_KV
        QPG = N_Q // N_KV
        ROPE_BASE = 10000.0
        WINDOW = 128
        EPS = 1.1920929e-07
        NEG = -1e+30

        def _rope(x, base=ROPE_BASE):
            t, d = (x.shape[-2], x.shape[-1])
            freqs = base ** (-2.0 * jnp.arange(d // 2, dtype=jnp.float32) / d)
            theta = jnp.arange(t, dtype=jnp.float32)[:, None] * freqs[None, :]
            cos, sin = (jnp.cos(theta), jnp.sin(theta))
            x1, x2 = (x[..., 0::2], x[..., 1::2])
            r1 = x1 * cos - x2 * sin
            r2 = x1 * sin + x2 * cos
            return jnp.stack([r1, r2], axis=-1).reshape(x.shape)

        def _rmsnorm(x, w):
            return x * jax.lax.rsqrt(jnp.mean(x * x, axis=-1, keepdims=True) + EPS) * w
        key = jax.random.key(seed)
        k0, k1, k2, k3 = jax.random.split(key, 4)
        x = jax.random.normal(k0, (B, T, D_MODEL), dtype=jnp.float32)
        wq = jax.random.normal(k1, (QPG * N_KV * D_HEAD, D_MODEL), dtype=jnp.float32) * 0.02
        wkv = jax.random.normal(k2, (2 * D_HEAD * N_KV, D_MODEL), dtype=jnp.float32) * 0.02
        wo = jax.random.normal(k3, (D_MODEL, D_HEAD * N_Q * N_KV), dtype=jnp.float32) * 0.02
        q_norm_w = jnp.ones((D_HEAD,), dtype=jnp.float32)
        k_norm_w = jnp.ones((D_HEAD,), dtype=jnp.float32)
        return {'x': x, 'wq': wq, 'wkv': wkv, 'wo': wo, 'q_norm_w': q_norm_w, 'k_norm_w': k_norm_w}
    _L0_attn_all = _L0_attn_setup()
    _L0_attn_in = {k: v for k, v in _L0_attn_all.items() if k in ('wq', 'wkv', 'wo', 'q_norm_w', 'k_norm_w')}
    del _L0_attn_all

    def _L0_ffn_setup():
        import jax, jax.numpy as jnp
        import numpy as np
        E = 8
        K = 2
        D = 64
        H = 128
        DOUT = 64
        EPS = 1e-05
        key = jax.random.key(seed)
        ks = jax.random.split(key, 9)
        s = 0.02
        return {'x': jax.random.normal(ks[0], (4, 2048, D), jnp.float32), 'gamma': 1.0 + 0.05 * jax.random.normal(ks[1], (D,), jnp.float32), 'beta': 0.05 * jax.random.normal(ks[2], (D,), jnp.float32), 'Wr': 0.01 * jax.random.normal(ks[3], (D, E), jnp.float32), 'br': jnp.zeros((E,), jnp.float32), 'W1': s * jax.random.normal(ks[4], (E, D, H), jnp.float32), 'b1': s * jax.random.normal(ks[5], (E, H), jnp.float32), 'W2': s * jax.random.normal(ks[6], (E, H, DOUT), jnp.float32), 'b2': s * jax.random.normal(ks[7], (E, DOUT), jnp.float32)}
    _L0_ffn_all = _L0_ffn_setup()
    _L0_ffn_in = {k: v for k, v in _L0_ffn_all.items() if k in ('gamma', 'beta', 'Wr', 'br', 'W1', 'b1', 'W2', 'b2')}
    del _L0_ffn_all
    return {'x': x, 'L0_tok_conv0_w': _L0_tok_in['conv0_w'], 'L0_tok_conv0_b': _L0_tok_in['conv0_b'], 'L0_tok_conv1_w': _L0_tok_in['conv1_w'], 'L0_tok_conv1_b': _L0_tok_in['conv1_b'], 'L0_tok_conv2_w': _L0_tok_in['conv2_w'], 'L0_tok_conv2_b': _L0_tok_in['conv2_b'], 'L0_tok_conv3_w': _L0_tok_in['conv3_w'], 'L0_tok_conv3_b': _L0_tok_in['conv3_b'], 'L0_tok_n0_w': _L0_tok_in['n0_w'], 'L0_tok_n0_b': _L0_tok_in['n0_b'], 'L0_tok_n1_w': _L0_tok_in['n1_w'], 'L0_tok_n1_b': _L0_tok_in['n1_b'], 'L0_tok_n2_w': _L0_tok_in['n2_w'], 'L0_tok_n2_b': _L0_tok_in['n2_b'], 'L0_tok_n3_w': _L0_tok_in['n3_w'], 'L0_tok_n3_b': _L0_tok_in['n3_b'], 'L0_tok_n4_w': _L0_tok_in['n4_w'], 'L0_tok_n4_b': _L0_tok_in['n4_b'], 'L0_tok_mlp_w1': _L0_tok_in['mlp_w1'], 'L0_tok_mlp_b1': _L0_tok_in['mlp_b1'], 'L0_tok_mlp_w2': _L0_tok_in['mlp_w2'], 'L0_tok_mlp_b2': _L0_tok_in['mlp_b2'], 'L0_tok_mlp_w3': _L0_tok_in['mlp_w3'], 'L0_tok_mlp_b3': _L0_tok_in['mlp_b3'], 'L0_attn_wq': _L0_attn_in['wq'], 'L0_attn_wkv': _L0_attn_in['wkv'], 'L0_attn_wo': _L0_attn_in['wo'], 'L0_attn_q_norm_w': _L0_attn_in['q_norm_w'], 'L0_attn_k_norm_w': _L0_attn_in['k_norm_w'], 'L0_ffn_gamma': _L0_ffn_in['gamma'], 'L0_ffn_beta': _L0_ffn_in['beta'], 'L0_ffn_Wr': _L0_ffn_in['Wr'], 'L0_ffn_br': _L0_ffn_in['br'], 'L0_ffn_W1': _L0_ffn_in['W1'], 'L0_ffn_b1': _L0_ffn_in['b1'], 'L0_ffn_W2': _L0_ffn_in['W2'], 'L0_ffn_b2': _L0_ffn_in['b2']}

def reference(x, L0_tok_conv0_w, L0_tok_conv0_b, L0_tok_conv1_w, L0_tok_conv1_b, L0_tok_conv2_w, L0_tok_conv2_b, L0_tok_conv3_w, L0_tok_conv3_b, L0_tok_n0_w, L0_tok_n0_b, L0_tok_n1_w, L0_tok_n1_b, L0_tok_n2_w, L0_tok_n2_b, L0_tok_n3_w, L0_tok_n3_b, L0_tok_n4_w, L0_tok_n4_b, L0_tok_mlp_w1, L0_tok_mlp_b1, L0_tok_mlp_w2, L0_tok_mlp_b2, L0_tok_mlp_w3, L0_tok_mlp_b3, L0_attn_wq, L0_attn_wkv, L0_attn_wo, L0_attn_q_norm_w, L0_attn_k_norm_w, L0_ffn_gamma, L0_ffn_beta, L0_ffn_Wr, L0_ffn_br, L0_ffn_W1, L0_ffn_b1, L0_ffn_W2, L0_ffn_b2):
    import jax
    import jax.numpy as jnp

    def _L0_tok_ref(x, conv0_w, conv0_b, conv1_w, conv1_b, conv2_w, conv2_b, conv3_w, conv3_b, n0_w, n0_b, n1_w, n1_b, n2_w, n2_b, n3_w, n3_b, n4_w, n4_b, mlp_w1, mlp_b1, mlp_w2, mlp_b2, mlp_w3, mlp_b3):
        import jax, jax.numpy as jnp
        import numpy as np
        B, L = (4, 10240)
        C = 128
        DMLP = 512
        TEMP = 1e-05
        EPS = 1e-05
        FACTOR = 2

        def _conv(x, w, b, stride, pad):
            x = jnp.pad(x, ((0, 0), (0, 0), (pad, pad)), mode='reflect')
            y = jax.lax.conv_general_dilated(x, w, (stride,), 'VALID', dimension_numbers=('NCH', 'OIH', 'NCH'))
            return y + b[None, :, None]

        def _cnorm(x, g, b):
            m = jnp.mean(x, axis=1, keepdims=True)
            v = jnp.var(x, axis=1, keepdims=True, ddof=1)
            return (x - m) * jax.lax.rsqrt(v + EPS) * g[None, :, None] + b[None, :, None]

        def _forward(x, conv0_w, conv0_b, conv1_w, conv1_b, conv2_w, conv2_b, conv3_w, conv3_b, n0_w, n0_b, n1_w, n1_b, n2_w, n2_b, n3_w, n3_b, n4_w, n4_b, mlp_w1, mlp_b1, mlp_w2, mlp_b2, mlp_w3, mlp_b3):
            h = jax.nn.relu(_cnorm(_conv(x, conv0_w, conv0_b, 5, 3), n0_w, n0_b))
            h = jax.nn.relu(_cnorm(_conv(h, conv1_w, conv1_b, 4, 2), n1_w, n1_b))
            h = jax.nn.relu(_cnorm(_conv(h, conv2_w, conv2_b, 2, 1), n2_w, n2_b))
            h = jax.nn.relu(_cnorm(_conv(h, conv3_w, conv3_b, 2, 1), n3_w, n3_b))
            f = jnp.transpose(h, (0, 2, 1))
            T = f.shape[1]
            z = jax.nn.gelu(f @ mlp_w1 + mlp_b1, approximate=False)
            z = jax.nn.gelu(z @ mlp_w2 + mlp_b2, approximate=False)
            imp = jax.nn.sigmoid((z @ mlp_w3 + mlp_b3)[..., 0]) + TEMP
            imp = imp / jnp.sum(imp, axis=1, keepdims=True) * (T / FACTOR)
            Tn = T // FACTOR
            cs = jnp.cumsum(imp, axis=1)
            p = jnp.maximum(cs[:, :, None] - jnp.arange(Tn, dtype=cs.dtype)[None, None, :], 0.0)
            pc = jnp.pad(p, ((0, 0), (0, 0), (0, 1)))
            d = pc[:, :, :-1] - pc[:, :, 1:]
            wmat = d - jnp.pad(d, ((0, 0), (1, 0), (0, 0)))[:, :-1, :]
            pooled = jnp.einsum('btn,btc->bnc', wmat, f)
            out = jnp.transpose(pooled, (0, 2, 1))
            return jax.nn.relu(_cnorm(out, n4_w, n4_b))
        return _forward(x, conv0_w, conv0_b, conv1_w, conv1_b, conv2_w, conv2_b, conv3_w, conv3_b, n0_w, n0_b, n1_w, n1_b, n2_w, n2_b, n3_w, n3_b, n4_w, n4_b, mlp_w1, mlp_b1, mlp_w2, mlp_b2, mlp_w3, mlp_b3)

    def _L0_attn_ref(x, wq, wkv, wo, q_norm_w, k_norm_w):
        import jax, jax.numpy as jnp
        import numpy as np
        import math
        B, T, D_MODEL = (1, 512, 64)
        N_Q, N_KV = (16, 1)
        D_HEAD = D_MODEL // N_KV
        QPG = N_Q // N_KV
        ROPE_BASE = 10000.0
        WINDOW = 128
        EPS = 1.1920929e-07
        NEG = -1e+30

        def _rope(x, base=ROPE_BASE):
            t, d = (x.shape[-2], x.shape[-1])
            freqs = base ** (-2.0 * jnp.arange(d // 2, dtype=jnp.float32) / d)
            theta = jnp.arange(t, dtype=jnp.float32)[:, None] * freqs[None, :]
            cos, sin = (jnp.cos(theta), jnp.sin(theta))
            x1, x2 = (x[..., 0::2], x[..., 1::2])
            r1 = x1 * cos - x2 * sin
            r2 = x1 * sin + x2 * cos
            return jnp.stack([r1, r2], axis=-1).reshape(x.shape)

        def _rmsnorm(x, w):
            return x * jax.lax.rsqrt(jnp.mean(x * x, axis=-1, keepdims=True) + EPS) * w
        Bx, Tx, C = x.shape
        q = x @ wq.T
        kv = x @ wkv.T
        k, v = (kv[..., :N_KV * D_HEAD], kv[..., N_KV * D_HEAD:])
        q = q.reshape(Bx, Tx, QPG, N_KV, D_HEAD).transpose(0, 2, 3, 1, 4)
        k = k.reshape(Bx, Tx, 1, N_KV, D_HEAD).transpose(0, 2, 3, 1, 4)
        v = v.reshape(Bx, Tx, 1, N_KV, D_HEAD).transpose(0, 2, 3, 1, 4)
        q = _rmsnorm(_rope(q), q_norm_w)
        k = _rmsnorm(_rope(k), k_norm_w)
        rows = jnp.arange(Tx)[:, None]
        cols = jnp.arange(Tx)[None, :]
        mask = (cols <= rows) & (rows - cols <= WINDOW)
        scale = 1.0 / math.sqrt(D_HEAD)
        scores = jnp.einsum('bqgtd,bqgsd->bqgts', q, k) * scale
        scores = jnp.where(mask[None, None, None], scores, NEG)
        attn = jax.nn.softmax(scores, axis=-1)
        out = jnp.einsum('bqgts,bqgsd->bqgtd', attn, v)
        out = out.transpose(0, 3, 1, 2, 4).reshape(Bx, Tx, QPG * N_KV * D_HEAD)
        return out @ wo.T

    def _L0_ffn_ref(x, gamma, beta, Wr, br, W1, b1, W2, b2):
        import jax, jax.numpy as jnp
        import numpy as np
        E = 8
        K = 2
        D = 64
        H = 128
        DOUT = 64
        EPS = 1e-05
        mu = jnp.mean(x, axis=-1, keepdims=True)
        var = jnp.mean(jnp.square(x - mu), axis=-1, keepdims=True)
        xn = (x - mu) * jax.lax.rsqrt(var + EPS) * gamma + beta
        logits = jnp.einsum('bsd,de->bse', xn, Wr) + br
        top_vals, top_idx = jax.lax.top_k(logits, K)
        w = jax.nn.softmax(top_vals, axis=-1)
        w_full = jnp.einsum('bsk,bske->bse', w, jax.nn.one_hot(top_idx, E, dtype=w.dtype))
        y = jnp.zeros(x.shape[:-1] + (DOUT,), x.dtype)
        for e in range(E):
            h = jax.nn.gelu(jnp.einsum('bsd,dh->bsh', xn, W1[e]) + b1[e], approximate=False)
            y_e = jnp.einsum('bsh,hd->bsd', h, W2[e]) + b2[e]
            y = y + y_e * w_full[..., e, None]
        return y
    h = _L0_tok_ref(x, L0_tok_conv0_w, L0_tok_conv0_b, L0_tok_conv1_w, L0_tok_conv1_b, L0_tok_conv2_w, L0_tok_conv2_b, L0_tok_conv3_w, L0_tok_conv3_b, L0_tok_n0_w, L0_tok_n0_b, L0_tok_n1_w, L0_tok_n1_b, L0_tok_n2_w, L0_tok_n2_b, L0_tok_n3_w, L0_tok_n3_b, L0_tok_n4_w, L0_tok_n4_b, L0_tok_mlp_w1, L0_tok_mlp_b1, L0_tok_mlp_w2, L0_tok_mlp_b2, L0_tok_mlp_w3, L0_tok_mlp_b3)
    h = h + _L0_attn_ref(_layernorm(h, axis=-1), L0_attn_wq, L0_attn_wkv, L0_attn_wo, L0_attn_q_norm_w, L0_attn_k_norm_w)
    h = h + _L0_ffn_ref(_layernorm(h, axis=-1), L0_ffn_gamma, L0_ffn_beta, L0_ffn_Wr, L0_ffn_br, L0_ffn_W1, L0_ffn_b1, L0_ffn_W2, L0_ffn_b2)
    return h

_drawn_inputs = setup_inputs


def setup_inputs(seed=0):
    import zlib

    import numpy as np

    out = dict(_drawn_inputs(seed))
    spreads = {'L0_tok_conv0_b': (0.0, 0.1),
     'L0_tok_conv1_b': (0.0, 0.1),
     'L0_tok_conv2_b': (0.0, 0.1),
     'L0_tok_conv3_b': (0.0, 0.1),
     'L0_tok_n0_w': (1.0, 0.2),
     'L0_tok_n0_b': (0.0, 0.1),
     'L0_tok_n1_w': (1.0, 0.2),
     'L0_tok_n1_b': (0.0, 0.1),
     'L0_tok_n2_w': (1.0, 0.2),
     'L0_tok_n2_b': (0.0, 0.1),
     'L0_tok_n3_w': (1.0, 0.2),
     'L0_tok_n3_b': (0.0, 0.1),
     'L0_tok_n4_w': (1.0, 0.2),
     'L0_tok_n4_b': (0.0, 0.1),
     'L0_tok_mlp_b1': (0.0, 0.487),
     'L0_tok_mlp_b2': (0.0, 0.342),
     'L0_attn_q_norm_w': (1.0, 0.6),
     'L0_attn_k_norm_w': (1.0, 0.6),
     'L0_ffn_br': (0.0, 0.322)}
    factors = {'L0_attn_wq': 2.863,
     'L0_ffn_gamma': 8.0,
     'L0_ffn_beta': 8.0,
     'L0_ffn_Wr': 5.796,
     'L0_ffn_W1': 3.896,
     'L0_ffn_b1': 8.0,
     'L0_ffn_W2': 3.853,
     'L0_ffn_b2': 3.713}
    for name, (base, spread) in spreads.items():
        noise = np.random.default_rng([zlib.crc32(name.encode()), seed]).standard_normal(out[name].shape)
        drawn = base * np.exp(spread * noise) if base else spread * noise
        out[name] = jnp.asarray(drawn.astype(out[name].dtype))
    for name, factor in factors.items():
        out[name] = (out[name] * factor).astype(out[name].dtype)
    return out
```

```python
from contextlib import ExitStack

import numpy as np

import concourse.bass as bass
from concourse import mybir

F32 = mybir.dt.float32
BF16 = mybir.dt.bfloat16
U32 = mybir.dt.uint32
ALU = mybir.AluOpType
ACT = mybir.ActivationFunctionType
AX_X = mybir.AxisListType.X

B = 64
L = 10240
C = 128
K0, ST0, PAD0 = 10, 5, 3
T0, T1, T2, T3 = 2048, 512, 256, 128
TN = T3 // 2
DMLP = 512
NH, DH = 16, 64
E, HID = 8, 128
EPS = 1e-5
EPS_RMS = 1.1920929e-07

PAIRS = B // 2
QUADS = B // 4
KR = K0 + 1
NG = 8
GR = NG * KR
GC = T0 // NG
PH0 = T1 + 1

CONSTS = [("ident", 128), ("cmat", 128), ("ones127", 128), ("gmask", 128), ("blkones", 128), ("tri", 128),
          ("stri", 128), ("ones", 128), ("mask", 128), ("iota", 64), ("cap", 64), ("ropec", 64), ("ropes", 64),
          ("iota8", 8)]
PARAMS = ["b1", "b2", "b3", "g0", "g1", "g2", "g3", "g4", "e0", "e1", "e2", "e3", "e4"]


def offsets(table):
    at, out = 0, {}
    for name, n in table:
        out[name] = (at, n)
        at += n
    return out, at


def pipeline(eng, count, stages, unroll=2):
    deepest = max(lag for _, lag in stages)
    first = deepest + 1 + (-(deepest + 1)) % unroll
    end = count - (count - first) % unroll

    def peeled(n):
        for f, lag in stages:
            if 0 <= n - lag < count:
                f(n - lag, n - lag)

    for n in range(first):
        peeled(n)
    with eng.Fori(first // unroll, end // unroll) as r:
        for u in range(unroll):
            for f, lag in stages:
                f(r * unroll + (u - lag), first + u - lag)
    for n in range(end, count + deepest):
        peeled(n)


def previous(order, count):
    lag = {s: g for s, g, _ in order}
    bank = {s: k for s, _, k in order}
    names = [s for s, _, _ in order]

    def prev(stage, i, lo):
        n = lo + lag[stage]
        before = names[:names.index(stage)]
        for m in range(n, -1, -1):
            for s in reversed(before):
                if bank[s] == bank[stage] and 0 <= m - lag[s] < count:
                    return s, i + (m - lag[s] - lo)
            before = names
        return None

    return prev


ORDER_CONV = [("conv1a", 2, "ya"), ("hT", 5, "aux"), ("conv0a0", 1, "y0a"), ("conv0a1", 1, "y0b"),
              ("statu", 0, "aux"), ("conv1b", 2, "yb"), ("var1a", 2, "var"), ("conv0b0", 1, "y0a"),
              ("conv0b1", 1, "y0b"), ("conv2", 3, "ya"), ("statv", 0, "var"), ("conv3", 4, "aux"),
              ("var1b", 2, "var"), ("var2", 3, "var"), ("var3", 4, "var")]
ORDER_MLP = [("m10", 0, "z0"), ("m20", 1, "w0"), ("m11", 0, "z1"), ("m21", 1, "w1"), ("m12", 0, "z0"),
             ("m22", 1, "w2"), ("m13", 0, "z1"), ("m23", 1, "w3"), ("m3", 2, "imp")]
ORDER_POOL = [("pool", 0, "p"), ("poolT", 1, "t")]
ORDER_ATT = [("q0", 1, "m0"), ("sc0", 2, "sa"), ("q1", 1, "m1"), ("pt0", 3, "p0"), ("pt1", 3, "p1"),
             ("kv", 1, "m0"), ("pv0", 3, "m1"), ("sc1", 2, "sb"), ("qt0", 1, "m0"), ("pt2", 3, "p0"),
             ("pt3", 3, "p1"), ("qt1", 1, "m1"), ("kt", 1, "m0"), ("pv1", 3, "m1"), ("wo", 3, "m0"),
             ("xt", 0, "m1")]
ORDER_ROUTE = [("xt", 1, "a"), ("lg", 2, "b")]
ORDER_EXP = [("w10", 0, "h0"), ("w27", 1, "y")] + [
    s for e in range(1, E) for s in ((f"w1{e}", 0, f"h{e % 2}"), (f"w2{e - 1}", 0, "y"))]


def stand_alone(ve, V):
    ve.tensor_copy(V["carrier"][:, 1:2], V["carrier"][:, 0:1])


def audio_tower(nc, A, out):
    const_at, n_const = offsets(CONSTS)
    with ExitStack() as ctx:
        def sb(name, shape, dt=F32):
            return ctx.enter_context(nc.sbuf_tensor(name, shape, dt))

        def sem(name):
            return ctx.enter_context(nc.semaphore(name))

        ps = ctx.enter_context(nc.psum_tensor("ps", [128, 8, 512], F32))

        const = sb("const", [128, n_const])
        K = {name: const[:, a:a + n] for name, (a, n) in const_at.items()}
        par = sb("par", [128, len(PARAMS)])
        P_ = {name: par[:, n:n + 1] for n, name in enumerate(PARAMS)}
        w0 = sb("w0", [GR, NG + 1, C])
        w123 = sb("w123", [128, 16, C])
        mw1 = sb("mw1", [128, DMLP])
        mw2 = sb("mw2", [128, 4, DMLP])
        mcol = sb("mcol", [128, 13])
        wqkv = sb("wqkv", [DH, NH * DH + 2 * DH])
        wo = sb("wo", [128, NH // 2, DH])
        qkw = sb("qkw", [128, 2 * DH])
        fcol = sb("fcol", [64, 2])
        fwr = sb("fwr", [DH, E])
        fbr = sb("fbr", [128, E])
        fw1 = sb("fw1", [DH, E, HID])
        fb1 = sb("fb1", [HID, E])
        fw2 = sb("fw2", [HID, E, DH])
        fb2 = sb("fb2", [128, E * DH])

        wmean = sb("wmean", [128, 16])
        w0mean = sb("w0mean", [GR, NG + 1])
        w0t = sb("w0t", [128, GR])
        gram = sb("gram", [GR, GR])
        bcen = sb("bcen", [128, 3])
        epsc = sb("epsc", [128, 2])
        carrier = sb("carrier", [128, 2])
        identb = sb("identb", [128, 128], BF16)
        maskb = sb("maskb", [128, 4, 128], BF16)
        wqk = sb("wqk", [128, DH])

        cs = sb("cs", [128, 2, B])
        mv = sb("mv", [128, B, 2])
        rstd = sb("rstd", [128, B])

        ld_const = sem("ld_const")
        ld_conv = sem("ld_conv")
        ld_late = sem("ld_late")
        su_v = sem("su_v")
        su_p = sem("su_p")

        with nc.Block() as block:
            @block.sync
            def _(sp):
                sp.dma_start(const[:], A["const"]).then_inc(ld_const, 16)
                sp.dma_start(par[:], A["par"]).then_inc(ld_const, 16)
                sp.dma_start(w0[:], A["w0"]).then_inc(ld_const, 16)
                sp.dma_start(w123[:], A["w123"]).then_inc(ld_conv, 16)
                for dst, name in ((mw1, "mw1"), (mw2, "mw2"), (mcol, "mcol"), (wqkv, "wqkv"), (wo, "wo"),
                                  (qkw, "qkw"), (fcol, "fcol"), (fwr, "fwr"), (fbr, "fbr"), (fw1, "fw1"),
                                  (fb1, "fb1"), (fw2, "fw2"), (fb2, "fb2")):
                    sp.dma_start(dst[:], A[name]).then_inc(ld_late, 16)
                sp.wait_ge(ld_late, 13 * 16)

            @block.vector
            def _(ve):
                ve.memset(epsc[:, 0:1], EPS).then_inc(su_v, 1)
                ve.memset(epsc[:, 1:2], EPS_RMS).then_inc(su_v, 1)
                ve.memset(carrier[:], 0.0)
                ve.wait_ge(ld_const, 48)
                ve.tensor_reduce(w0mean[:], w0[:], AX_X, ALU.add).then_inc(su_v, 1)
                ve.wait_ge(su_v, 3)
                ve.tensor_scalar(w0mean[:], w0mean[:], 1.0 / C, None, ALU.mult).then_inc(su_v, 1)
                ve.wait_ge(su_v, 4)
                ve.tensor_tensor(w0[:], w0[:], w0mean[:].unsqueeze(2).to_broadcast([GR, NG + 1, C]),
                                 ALU.subtract).then_inc(su_v, 1)
                ve.tensor_copy(identb[:], K["ident"]).then_inc(su_v, 1)
                ve.tensor_copy(maskb[:], K["mask"].unsqueeze(1).to_broadcast([128, 4, 128])).then_inc(su_v, 1)
                ve.wait_ge(ld_conv, 16)
                ve.tensor_reduce(wmean[:], w123[:], AX_X, ALU.add).then_inc(su_v, 1)
                ve.wait_ge(su_v, 8)
                ve.tensor_scalar(wmean[:], wmean[:], 1.0 / C, None, ALU.mult).then_inc(su_v, 1)
                ve.wait_ge(su_v, 9)
                ve.tensor_tensor(w123[:], w123[:], wmean[:].unsqueeze(2).to_broadcast([128, 16, C]),
                                 ALU.subtract).then_inc(su_v, 1)
                ve.wait_ge(su_p, 1)
                ve.tensor_copy(w0t[:], ps[:, 0, 0:GR]).then_inc(su_v, 1)
                ve.wait_ge(su_p, 2)
                ve.tensor_copy(bcen[:], ps[:, 1, 0:3]).then_inc(su_v, 1)
                ve.wait_ge(su_p, 3)
                ve.tensor_tensor(gram[:], ps[0:GR, 2, 0:GR], K["gmask"][0:GR, 0:GR], ALU.mult).then_inc(su_v, 1)
                ve.wait_ge(ld_late, 13 * 16)
                ve.scalar_tensor_tensor(out=wqk[:], in0=qkw[:, 0:DH], scalar=float(DH) ** -0.5,
                                        in1=qkw[:, DH:2 * DH], op0=ALU.mult, op1=ALU.mult).then_inc(su_v, 1)
                ve.wait_ge(su_v, 14)

            @block.tensor
            def _(pe):
                pe.wait_ge(ld_const, 48)
                pe.wait_ge(su_v, 5)
                pe.transpose(ps[:, 0, 0:GR], w0[:, NG, :], K["ident"][0:GR, 0:GR]).then_inc(su_p, 1)
                pe.matmul(ps[:, 1, 0:3], K["cmat"], par[:, 0:3], start=True, stop=True).then_inc(su_p, 1)
                pe.wait_ge(su_v, 11)
                pe.matmul(ps[0:GR, 2, 0:GR], w0t[:], w0t[:], start=True, stop=True).then_inc(su_p, 1)

        V = dict(carrier=carrier, ps=ps, K=K, P=P_, w0=w0, w123=w123, gram=gram, bcen=bcen, epsc=epsc, mw1=mw1, mw2=mw2, mcol=mcol,
                 cs=cs, mv=mv, rstd=rstd, wqkv=wqkv, wo=wo, wqk=wqk, identb=identb, maskb=maskb, fcol=fcol, fwr=fwr,
                 fbr=fbr, fw1=fw1, fb1=fb1, fw2=fw2, fb2=fb2)
        with ExitStack() as tok:
            V["hT"] = tok.enter_context(nc.sbuf_tensor("hT", [128, B * C], F32))
            with ExitStack() as mlp:
                V["h3"] = mlp.enter_context(nc.sbuf_tensor("h3", [128, B * T3], F32))
                early = tok.enter_context(ExitStack())
                numbers = []

                def early_sem(name):
                    handle = early.enter_context(nc.semaphore(name))
                    numbers.append(handle.num)
                    return handle

                conv_phase(nc, A, V, early_sem)
                importance_phase(nc, V, early_sem)
            V["h4"] = tok.enter_context(nc.sbuf_tensor("h4", [128, B, TN], F32))
            pool_phase(nc, V, sem)
            attention_phase(nc, V, sem)
            early.close()
            with nc.Block() as block:
                @block.gpsimd
                def _(po):
                    po.sem_clear(range(min(numbers), max(numbers) + 1))
            ffn_phase(nc, V, out, sem)


def conv_phase(nc, A, V, sem):
    ps, K, P_, epsc, bcen = V["ps"], V["K"], V["P"], V["epsc"], V["bcen"]
    w0, w123, gram, hT, h3 = V["w0"], V["w123"], V["gram"], V["hT"], V["h3"]
    prev = previous(ORDER_CONV, PAIRS)
    with ExitStack() as ctx:
        def sb(name, shape, dt=F32):
            return ctx.enter_context(nc.sbuf_tensor(name, shape, dt))

        x8 = sb("x8", [GR, 2, 2 * GC])
        xs = sb("xs", [GR, 2, 2 * GC])
        h0 = sb("h0", [128, 2, 2, 4 * PH0])
        h1 = sb("h1", [128, 2, 2, T1 + 2])
        h2 = sb("h2", [128, 2, 2, T2 + 2])
        h3s = sb("h3s", [128, 2, 2, T3])
        gx = sb("gx", [GR, 2 * GC])
        ln0 = sb("ln0", [GR, 2 * GC])
        r0 = sb("r0", [GR, 2 * GC])
        NORMS = ("1a", "1b", "2", "3")
        WIDTH = {"1a": T1, "1b": T1, "2": 2 * T2, "3": 2 * T3}
        BIAS = {"1a": 0, "1b": 0, "2": 1, "3": 2}
        sq = {s: sb("sq" + s, [128, WIDTH[s]]) for s in NORMS}
        lnv = {s: sb("ln" + s, [128, WIDTH[s]]) for s in NORMS}
        rs = {s: sb("rs" + s, [128, WIDTH[s]]) for s in NORMS}
        yn = {s: sb("yn" + s, [128, WIDTH[s]]) for s in NORMS}

        ld_x = [sem("ld_x0"), sem("ld_x1")]
        filled = {s: sem("cf_" + s) for s, _, _ in ORDER_CONV}
        s_gx = sem("s_gx")
        s_ln0 = sem("s_ln0")
        s_r0 = sem("s_r0")
        s_xs = sem("s_xs")
        s_h0 = {s: sem("s_h" + s) for s in ("conv0a0", "conv0a1", "conv0b0", "conv0b1")}
        s_pad0 = [sem("s_pad0a"), sem("s_pad0b")]
        s_sq = {s: sem("s_sq" + s) for s in NORMS}
        s_ln = {s: sem("s_ln" + s) for s in NORMS}
        s_rs = {s: sem("s_rs" + s) for s in NORMS}
        s_yn = {s: sem("s_yn" + s) for s in NORMS}
        s_act = {s: sem("s_act" + s) for s in NORMS}
        s_pad1 = sem("s_pad1")
        s_pad2 = sem("s_pad2")
        s_hT = sem("s_hT")
        s_keep = sem("s_keep")
        read = {"conv1a": s_yn["1a"], "conv1b": s_yn["1b"], "conv2": s_yn["2"], "conv3": s_yn["3"],
                "var1a": s_ln["1a"], "var1b": s_ln["1b"], "var2": s_ln["2"], "var3": s_ln["3"],
                "statu": s_gx, "statv": s_ln0, "hT": s_hT, **s_h0}
        YB = {"1a": ps[:, 4, :], "1b": ps[:, 5, :], "2": ps[:, 4, :], "3": ps[:, 7, 0:2 * T3]}

        with nc.Block() as block:
            @block.sync
            def _(sp):
                def load(i, lo):
                    if lo >= 2:
                        sp.wait_ge(s_xs, i - 1)
                    sp.dma_start(x8[:, lo % 2, :], A["x8"][bass.ds(i * GR, GR), :]).then_inc(ld_x[lo % 2], 16)

                pipeline(sp, PAIRS, [(load, 0)])

            @block.tensor
            def _(pe):
                def bank_free(stage, i, lo):
                    p = prev(stage, i, lo)
                    if p:
                        pe.wait_ge(read[p[0]], p[1] + 1)

                def statu(i, lo):
                    bank_free("statu", i, lo)
                    pe.wait_ge(ld_x[lo % 2], i * 8 + (16 - 8 * (lo % 2)))
                    pe.matmul(ps[0:GR, 7, :], gram[:], x8[:, lo % 2, :], start=True,
                              stop=True).then_inc(filled["statu"], 1)

                def statv(i, lo):
                    bank_free("statv", i, lo)
                    pe.wait_ge(s_gx, i + 1)
                    pe.matmul(ps[0:GR, 6, :], K["blkones"][0:GR, 0:GR], gx[:], start=True,
                              stop=True).then_inc(filled["statv"], 1)

                def conv0(row, half):
                    stage = "conv0" + "ab"[row] + "01"[half]

                    def f(i, lo):
                        bank_free(stage, i, lo)
                        pe.wait_ge(s_xs, i + 1)
                        for q in (2 * half, 2 * half + 1):
                            for g in range(2):
                                last = pe.matmul(ps[:, q, g * GC:(g + 1) * GC], w0[:, 2 * q + g, :],
                                                 xs[:, lo % 2, row * GC:(row + 1) * GC], start=True, stop=True)
                        last.then_inc(filled[stage], 1)
                    return f

                def conv1(row):
                    stage = "conv1" + "ab"[row]

                    def f(i, lo):
                        bank_free(stage, i, lo)
                        pe.wait_ge(s_pad0[row], i + 1)
                        for t in range(8):
                            a, q = t // 4, t % 4
                            last = pe.matmul(ps[:, 4 + row, :], w123[:, t, :],
                                             h0[:, lo % 2, row, q * PH0 + a:q * PH0 + a + T1],
                                             start=(t == 0), stop=(t == 7))
                        last.then_inc(filled[stage], 1)
                    return f

                def conv23(stage, h, w_at, n_out, bank, padded):
                    def f(i, lo):
                        bank_free(stage, i, lo)
                        pe.wait_ge(padded, i + 1)
                        for t in range(4):
                            at = (t % 2) * (n_out + 1) + t // 2
                            last = pe.matmul(ps[:, bank, 0:2 * n_out].rearrange("p (r t) -> p r t", r=2),
                                             w123[:, w_at + t, :], h[:, lo % 2, :, at:at + n_out],
                                             start=(t == 0), stop=(t == 3))
                        last.then_inc(filled[stage], 1)
                    return f

                def var(s):
                    def f(i, lo):
                        bank_free("var" + s, i, lo)
                        pe.wait_ge(s_sq[s], i + 1)
                        pe.matmul(ps[:, 6, 0:WIDTH[s]], K["ones127"], sq[s][:], start=True,
                                  stop=True).then_inc(filled["var" + s], 1)
                    return f

                def trans(i, lo):
                    bank_free("hT", i, lo)
                    pe.wait_ge(s_act["3"], i + 1)
                    for row in range(2):
                        last = pe.transpose(ps[:, 7, row * C:(row + 1) * C], h3s[:, lo % 2, row, :], K["ident"])
                    last.then_inc(filled["hT"], 1)

                stages = {"conv1a": conv1(0), "hT": trans, "conv0a0": conv0(0, 0), "conv0a1": conv0(0, 1),
                          "statu": statu, "conv1b": conv1(1), "var1a": var("1a"), "conv0b0": conv0(1, 0),
                          "conv0b1": conv0(1, 1), "conv2": conv23("conv2", h1, 8, T2, 4, s_pad1), "statv": statv,
                          "conv3": conv23("conv3", h2, 12, T3, 7, s_pad2), "var1b": var("1b"), "var2": var("2"),
                          "var3": var("3")}
                pipeline(pe, PAIRS, [(stages[s], lag) for s, lag, _ in ORDER_CONV])

            @block.scalar
            def _(ac):
                ac.preload_act_table_set("natural_log_exp_and_others")

                def relu0(row, half):
                    stage = "conv0" + "ab"[row] + "01"[half]

                    def f(i, lo):
                        ac.wait_ge(filled[stage], i + 1)
                        if lo >= 2:
                            ac.wait_ge(filled["conv1" + "ab"[row]], i - 1)
                        o = h0[:, lo % 2, row, 2 * half * PH0:2 * (half + 1) * PH0].rearrange(
                            "p (q t) -> p q t", q=2)[:, :, 1 - half:1 - half + T1]
                        ac.activation(o, ps[:, 2 * half:2 * half + 2, :], ACT.Relu, bias=P_["e0"],
                                      scale=P_["g0"]).then_inc(s_h0[stage], 1)
                    return f

                def square(s, stage):
                    def f(i, lo):
                        ac.wait_ge(filled[stage], i + 1)
                        if lo >= 1:
                            ac.wait_ge(filled["var" + s], i)
                        ac.activation(sq[s][:], YB[s], ACT.Square, bias=bcen[:, BIAS[s]:BIAS[s] + 1]
                                      ).then_inc(s_sq[s], 1)
                    return f

                def rsqrt(s):
                    def f(i, lo):
                        ac.wait_ge(filled["var" + s], i + 1)
                        ac.activation(lnv[s][:], ps[:, 6, 0:WIDTH[s]], ACT.Ln, bias=epsc[:, 0:1]
                                      ).then_inc(s_ln[s], 1)
                        if lo >= 1:
                            ac.wait_ge(s_yn[s], i)
                        ac.wait_ge(s_ln[s], i + 1)
                        ac.activation(rs[s][:], lnv[s][:], ACT.Exp, scale=-0.5).then_inc(s_rs[s], 1)
                    return f

                def rsqrt0(i, lo):
                    ac.wait_ge(filled["statv"], i + 1)
                    ac.activation(ln0[:], ps[0:GR, 6, :], ACT.Ln, bias=epsc[0:GR, 0:1]).then_inc(s_ln0, 1)
                    if lo >= 1:
                        ac.wait_ge(s_xs, i)
                    ac.wait_ge(s_ln0, i + 1)
                    ac.activation(r0[:], ln0[:], ACT.Exp, scale=-0.5).then_inc(s_r0, 1)

                def relu1(row):
                    s = "1" + "ab"[row]

                    def f(i, lo):
                        ac.wait_ge(s_yn[s], i + 1)
                        if lo >= 2:
                            ac.wait_ge(filled["conv2"], i - 1)
                        for odd in (1, 0):
                            at = 1 if odd else 1 + T2
                            last = ac.activation(h1[:, lo % 2, row, at:at + T2], yn[s][:, odd::2], ACT.Relu,
                                                 bias=P_["e1"], scale=P_["g1"])
                        last.then_inc(s_act[s], 1)
                    return f

                def relu2(i, lo):
                    ac.wait_ge(s_yn["2"], i + 1)
                    if lo >= 2:
                        ac.wait_ge(filled["conv3"], i - 1)
                    y = yn["2"][:].rearrange("p (r t) -> p r t", r=2)
                    for odd in (1, 0):
                        at = 1 if odd else 1 + T3
                        last = ac.activation(h2[:, lo % 2, :, at:at + T3], y[:, :, odd::2], ACT.Relu,
                                             bias=P_["e2"], scale=P_["g2"])
                    last.then_inc(s_act["2"], 1)

                def relu3(i, lo):
                    ac.wait_ge(s_yn["3"], i + 1)
                    if lo >= 2:
                        ac.wait_ge(filled["hT"], i - 1)
                        ac.wait_ge(s_keep, i - 1)
                    ac.activation(h3s[:, lo % 2, :, :], yn["3"][:].rearrange("p (r t) -> p r t", r=2),
                                  ACT.Relu, bias=P_["e3"], scale=P_["g3"]).then_inc(s_act["3"], 1)

                pipeline(ac, PAIRS, [(square("1a", "conv1a"), 2), (relu0(0, 0), 1), (relu0(0, 1), 1),
                                     (square("1b", "conv1b"), 2), (rsqrt("1a"), 2), (relu0(1, 0), 1),
                                     (relu0(1, 1), 1), (relu1(0), 2), (square("2", "conv2"), 3), (rsqrt0, 0),
                                     (square("3", "conv3"), 4), (rsqrt("1b"), 2), (rsqrt("2"), 3), (relu1(1), 2),
                                     (rsqrt("3"), 4), (relu2, 3), (relu3, 4)])

            @block.vector
            def _(ve):
                def keep_t(i, lo):
                    ve.wait_ge(filled["hT"], i + 1)
                    ve.tensor_copy(hT[:, bass.ds(i * (2 * C), 2 * C)], ps[:, 7, 0:2 * C]).then_inc(s_hT, 1)

                def keep(i, lo):
                    ve.wait_ge(s_act["3"], i + 1)
                    ve.tensor_copy(h3[:, bass.ds(i * (2 * T3), 2 * T3)],
                                   h3s[:, lo % 2, :, :].rearrange("p r t -> p (r t)")).then_inc(s_keep, 1)

                def product(i, lo):
                    ve.wait_ge(filled["statu"], i + 1)
                    if lo >= 1:
                        ve.wait_ge(filled["statv"], i)
                    ve.tensor_tensor(gx[:], ps[0:GR, 7, :], x8[:, lo % 2, :], ALU.mult).then_inc(s_gx, 1)

                def scaled(i, lo):
                    ve.wait_ge(s_r0, i + 1)
                    if lo >= 2:
                        ve.wait_ge(filled["conv0b1"], i - 1)
                    ve.tensor_tensor(xs[:, lo % 2, :], x8[:, lo % 2, :], r0[:], ALU.mult).then_inc(s_xs, 1)

                def norm(s):
                    def f(i, lo):
                        ve.wait_ge(s_rs[s], i + 1)
                        if lo >= 1:
                            ve.wait_ge(s_act[s], i)
                        ve.scalar_tensor_tensor(out=yn[s][:], in0=YB[s], scalar=bcen[:, BIAS[s]:BIAS[s] + 1],
                                                in1=rs[s][:], op0=ALU.add, op1=ALU.mult).then_inc(s_yn[s], 1)
                    return f

                pipeline(ve, PAIRS, [(keep_t, 5), (keep, 5), (product, 0), (norm("1a"), 2), (scaled, 0),
                                     (norm("1b"), 2), (norm("2"), 3), (norm("3"), 4)])

            @block.gpsimd
            def _(po):
                def pad0(row):
                    def f(i, lo):
                        po.wait_ge(s_h0["conv0" + "ab"[row] + "0"], i + 1)
                        po.wait_ge(s_h0["conv0" + "ab"[row] + "1"], i + 1)
                        h = h0[:, lo % 2, row, :]
                        for to, frm in ((0, 1), (PH0, 3 * PH0), (3 * PH0 - 1, PH0 - 1), (4 * PH0 - 1, 4 * PH0 - 2)):
                            e = h[:, frm:frm + 1]
                            last = po.tensor_tensor(h[:, to:to + 1], e, K["ones"][:, 0:1], ALU.mult)
                        last.then_inc(s_pad0[row], 1)
                    return f

                def pad1(i, lo):
                    po.wait_ge(s_act["1a"], i + 1)
                    po.wait_ge(s_act["1b"], i + 1)
                    one = K["ones"][:, 0:2].unsqueeze(2)
                    front, back = h1[:, lo % 2, :, 1:2], h1[:, lo % 2, :, T1:T1 + 1]
                    po.tensor_tensor(h1[:, lo % 2, :, 0:1], front, one, ALU.mult)
                    po.tensor_tensor(h1[:, lo % 2, :, T1 + 1:T1 + 2], back, one, ALU.mult).then_inc(s_pad1, 1)

                def pad2(i, lo):
                    po.wait_ge(s_act["2"], i + 1)
                    one = K["ones"][:, 0:2].unsqueeze(2)
                    front, back = h2[:, lo % 2, :, 1:2], h2[:, lo % 2, :, T2:T2 + 1]
                    po.tensor_tensor(h2[:, lo % 2, :, 0:1], front, one, ALU.mult)
                    po.tensor_tensor(h2[:, lo % 2, :, T2 + 1:T2 + 2], back, one, ALU.mult).then_inc(s_pad2, 1)

                pipeline(po, PAIRS, [(pad0(0), 1), (pad0(1), 1), (pad1, 2), (pad2, 3)])


def importance_phase(nc, V, sem):
    ps, K, h3, cs = V["ps"], V["K"], V["h3"], V["cs"]
    mw1, mw2, mcol = V["mw1"], V["mw2"], V["mcol"]
    NT = 4 * T3
    prev = previous(ORDER_MLP, QUADS)
    with ExitStack() as ctx:
        def sb(name, shape, dt=F32):
            return ctx.enter_context(nc.sbuf_tensor(name, shape, dt))

        z1 = sb("z1", [128, 2, 4, NT])
        z2 = sb("z2", [128, 2, 4, NT])
        imp = sb("imp", [128, B])
        impn = sb("impn", [128, B])
        rtot = sb("rtot", [128, B])
        filled = {s: sem("mf_" + s) for s, _, _ in ORDER_MLP}
        s_z1 = [sem(f"s_z1{m}") for m in range(4)]
        s_z2 = [sem(f"s_z2{m}") for m in range(4)]
        s_sig, s_imp, s_tot, s_cum = sem("s_sig"), sem("s_imp"), sem("s_tot"), sem("s_cum")
        read = {**{f"m1{m}": s_z1[m] for m in range(4)}, **{f"m2{m}": s_z2[m] for m in range(4)}}

        with nc.Block() as block:
            @block.tensor
            def _(pe):
                def layer1(m):
                    def f(i, lo):
                        p = prev(f"m1{m}", i, lo)
                        if p:
                            pe.wait_ge(read[p[0]], p[1] + 1)
                        pe.matmul(ps[:, m % 2, :], mw1[:, m * 128:(m + 1) * 128], h3[:, bass.ds(i * NT, NT)],
                                  start=True, stop=True).then_inc(filled[f"m1{m}"], 1)
                    return f

                def layer2(m):
                    def f(i, lo):
                        p = prev(f"m2{m}", i, lo)
                        if p:
                            pe.wait_ge(read[p[0]], p[1] + 1)
                        if m == 0:
                            pe.wait_ge(s_z1[3], i + 1)
                        for k in range(4):
                            last = pe.matmul(ps[:, 2 + m, :], mw2[:, k, m * 128:(m + 1) * 128], z1[:, lo % 2, k, :],
                                             start=(k == 0), stop=(k == 3))
                        last.then_inc(filled[f"m2{m}"], 1)
                    return f

                def layer3(i, lo):
                    pe.wait_ge(s_z2[3], i + 1)
                    for r in range(4):
                        for k in range(4):
                            last = pe.matmul(ps[:, 6, bass.ds(4 * i + r, 1)], z2[:, lo % 2, k, r * T3:(r + 1) * T3],
                                             mcol[:, 8 + k:9 + k], start=(k == 0), stop=(k == 3))
                    last.then_inc(filled["m3"], 1)

                stages = {**{f"m1{m}": layer1(m) for m in range(4)}, **{f"m2{m}": layer2(m) for m in range(4)},
                          "m3": layer3}
                pipeline(pe, QUADS, [(stages[s], lag) for s, lag, _ in ORDER_MLP])
                pe.wait_ge(s_imp, 1)
                pe.matmul(ps[:, 0, 0:B], K["ones"], imp[:], start=True, stop=True).then_inc(s_tot, 1)
                pe.wait_ge(s_imp, 3)
                pe.matmul(ps[:, 1, 0:B], K["stri"], impn[:], start=True, stop=True)
                pe.matmul(ps[:, 1, B:2 * B], K["tri"], impn[:], start=True, stop=True).then_inc(s_tot, 1)

            @block.scalar
            def _(ac):
                def gelu1(m):
                    def f(i, lo):
                        ac.wait_ge(filled[f"m1{m}"], i + 1)
                        if lo >= 2:
                            ac.wait_ge(filled["m23"], i - 1)
                        ac.activation(z1[:, lo % 2, m, :], ps[:, m % 2, :], ACT.Gelu,
                                      bias=mcol[:, m:m + 1]).then_inc(s_z1[m], 1)
                    return f

                def gelu2(m):
                    def f(i, lo):
                        ac.wait_ge(filled[f"m2{m}"], i + 1)
                        if lo >= 2:
                            ac.wait_ge(filled["m3"], i - 1)
                        ac.activation(z2[:, lo % 2, m, :], ps[:, 2 + m, :], ACT.Gelu,
                                      bias=mcol[:, 4 + m:5 + m]).then_inc(s_z2[m], 1)
                    return f

                ac.preload_act_table_set("gelu_and_others")
                pipeline(ac, QUADS, [s for m in range(4) for s in ((gelu1(m), 0), (gelu2(m), 1))])
                ac.wait_ge(filled["m3"], QUADS)
                ac.activation(imp[:], ps[:, 6, 0:B], ACT.Sigmoid, bias=mcol[:, 12:13]).then_inc(s_sig, 1)

            @block.vector
            def _(ve):
                ve.wait_ge(s_sig, 1)
                ve.tensor_scalar(imp[:], imp[:], EPS, None, ALU.add).then_inc(s_imp, 1)
                ve.wait_ge(s_tot, 1)
                ve.reciprocal(rtot[:], ps[:, 0, 0:B]).then_inc(s_imp, 1)
                ve.wait_ge(s_imp, 2)
                ve.scalar_tensor_tensor(out=impn[:], in0=imp[:], scalar=float(TN), in1=rtot[:], op0=ALU.mult,
                                        op1=ALU.mult).then_inc(s_imp, 1)
                ve.wait_ge(s_tot, 2)
                ve.tensor_copy(cs[:], ps[:, 1, 0:2 * B].rearrange("p (k b) -> p k b", k=2)).then_inc(s_cum, 1)
                ve.wait_ge(s_cum, 1)


def pool_phase(nc, V, sem):
    ps, K, P_, epsc = V["ps"], V["K"], V["P"], V["epsc"]
    hT, cs, h4, mv, rstd = V["hT"], V["cs"], V["h4"], V["mv"], V["rstd"]
    prev = previous(ORDER_POOL, PAIRS)
    with ExitStack() as ctx:
        def sb(name, shape, dt=F32):
            return ctx.enter_context(nc.sbuf_tensor(name, shape, dt))

        part = sb("part", [128, 4, TN])
        wm = sb("wm", [128, 2, 384])
        st = sb("pst", [128, 6])
        pm = sb("pm", [128, 2, 2])
        lr = sb("plr", [128, 1])
        pr = sb("pr", [128, 2])
        xh = sb("xh", [128, 2, C])
        st4 = sb("pst4", [128, 2, 6])
        mvs = sb("pmvs", [128, 2, 2])
        lrs = sb("plrs", [128, B])
        filled = {s: sem("pf_" + s) for s, _, _ in ORDER_POOL}
        s_zero, s_part, s_wm, s_st, s_pm, s_lr, s_pr = (sem("p_" + n) for n in
                                                         ("zero", "part", "wm", "st", "pm", "lr", "pr"))
        s_xh, s_h4, s_st4, s_mv, s_all = (sem("p_" + n) for n in ("xh", "h4", "st4", "mv", "all"))
        read = {"pool": s_xh, "poolT": s_h4}

        with nc.Block() as block:
            @block.tensor
            def _(pe):
                def pool(i, lo):
                    p = prev("pool", i, lo)
                    if p:
                        pe.wait_ge(read[p[0]], p[1] + 1)
                    pe.wait_ge(s_wm, i + 1)
                    for r in range(2):
                        last = pe.matmul(ps[:, 0, 0:C], wm[:, lo % 2, r * 128:(r + 1) * 128],
                                         hT[:, bass.ds(i * (2 * C) + r * C, C)], start=(r == 0), stop=(r == 1))
                    last.then_inc(filled["pool"], 1)

                def pool_t(i, lo):
                    p = prev("poolT", i, lo)
                    if p:
                        pe.wait_ge(read[p[0]], p[1] + 1)
                    pe.wait_ge(s_xh, i + 1)
                    pe.transpose(ps[:, 1, 0:128], xh[:, lo % 2, :], K["ident"]).then_inc(filled["poolT"], 1)

                pipeline(pe, PAIRS, [(pool, 0), (pool_t, 1)])

            @block.vector
            def _(ve):
                def weights(i, lo):
                    if lo >= 1:
                        ve.wait_ge(s_wm, i)
                    ve.tensor_tensor(part[:].rearrange("p (k r) n -> p k r n", k=2),
                                     cs[:, :, bass.ds(2 * i, 2)].unsqueeze(3).to_broadcast([128, 2, 2, TN]),
                                     K["iota"].unsqueeze(1).unsqueeze(1).to_broadcast([128, 2, 2, TN]),
                                     ALU.subtract).then_inc(s_part, 1)
                    ve.wait_ge(s_part, 2 * i + 1)
                    ve.scalar_tensor_tensor(out=part[:], in0=part[:], scalar=0.0,
                                            in1=K["cap"].unsqueeze(1).to_broadcast([128, 4, TN]), op0=ALU.max,
                                            op1=ALU.min).then_inc(s_part, 1)
                    ve.wait_ge(s_part, 2 * i + 2)
                    if lo >= 2:
                        ve.wait_ge(filled["pool"], i - 1)
                    ve.tensor_tensor(wm[:, lo % 2, :].rearrange("p (r n) -> p r n", r=2)[:, :, 0:TN],
                                     part[:, 2:4, :], part[:, 0:2, :], ALU.subtract).then_inc(s_wm, 1)

                def stats(i, lo):
                    ve.wait_ge(filled["pool"], i + 1)
                    if lo >= 1:
                        ve.wait_ge(s_pm, i)
                    ve.bn_stats(st[:], ps[:, 0, 0:C]).then_inc(s_st, 1)
                    if lo >= 2:
                        ve.wait_ge(s_xh, i - 1)
                    ve.wait_ge(s_st, i + 1)
                    stand_alone(ve, V)
                    ve.bn_aggr(pm[:, lo % 2, :], st[:]).then_inc(s_pm, 1)

                def whiten(i, lo):
                    ve.wait_ge(s_pr, i + 1)
                    if lo >= 2:
                        ve.wait_ge(filled["poolT"], i - 1)
                    ve.tensor_scalar(xh[:, lo % 2, :], ps[:, 0, 0:C], pm[:, lo % 2, 0:1], pr[:, lo % 2:lo % 2 + 1],
                                     ALU.subtract, ALU.mult).then_inc(s_xh, 1)

                def stats4(i, lo):
                    ve.wait_ge(s_h4, i + 1)
                    if lo >= 1:
                        ve.wait_ge(s_mv, 2 * i)
                    stand_alone(ve, V)
                    for r in range(2):
                        last = ve.bn_stats(st4[:, r, :], h4[:, bass.ds(2 * i + r, 1), :].rearrange("p a n -> p (a n)"))
                    last.then_inc(s_st4, 1)
                    ve.wait_ge(s_st4, i + 1)
                    stand_alone(ve, V)
                    for r in range(2):
                        last = ve.bn_aggr(mvs[:, r, :], st4[:, r, :])
                    last.then_inc(s_mv, 1)
                    ve.wait_ge(s_mv, 2 * i + 1)
                    ve.tensor_copy(mv[:, bass.ds(2 * i, 2), :], mvs[:]).then_inc(s_mv, 1)

                ve.memset(wm[:], 0.0).then_inc(s_zero, 1)
                ve.wait_ge(s_zero, 1)
                pipeline(ve, PAIRS, [(weights, 0), (stats, 0), (whiten, 0), (stats4, 2)])
                ve.wait_ge(s_all, 1)

            @block.scalar
            def _(ac):
                ac.preload_act_table_set("natural_log_exp_and_others")

                def rsqrt(i, lo):
                    ac.wait_ge(s_pm, i + 1)
                    ac.activation(lr[:], pm[:, lo % 2, 1:2], ACT.Ln, bias=epsc[:, 0:1],
                                  scale=float(C) / (C - 1)).then_inc(s_lr, 1)
                    if lo >= 2:
                        ac.wait_ge(s_xh, i - 1)
                    ac.wait_ge(s_lr, i + 1)
                    ac.activation(pr[:, lo % 2:lo % 2 + 1], lr[:], ACT.Exp, scale=-0.5).then_inc(s_pr, 1)

                def relu(i, lo):
                    ac.wait_ge(filled["poolT"], i + 1)
                    ac.activation(h4[:, bass.ds(2 * i, 2), :], ps[:, 1, 0:128].rearrange("p (r n) -> p r n", r=2),
                                  ACT.Relu, bias=P_["e4"], scale=P_["g4"]).then_inc(s_h4, 1)

                pipeline(ac, PAIRS, [(rsqrt, 0), (relu, 1)])
                ac.wait_ge(s_mv, 2 * PAIRS)
                ac.activation(lrs[:], mv[:, :, 1], ACT.Ln, bias=epsc[:, 0:1]).then_inc(s_all, 1)
                ac.wait_ge(s_all, 1)
                ac.activation(rstd[:], lrs[:], ACT.Exp, scale=-0.5).then_inc(s_all, 1)
                ac.wait_ge(s_all, 2)


def attention_phase(nc, V, sem):
    ps, K, epsc = V["ps"], V["K"], V["epsc"]
    h4, mv, rstd = V["h4"], V["mv"], V["rstd"]
    wqkv, wo, wqk, identb, maskb = V["wqkv"], V["wo"], V["wqk"], V["identb"], V["maskb"]
    T, QK = C, NH * DH
    prev = previous(ORDER_ATT, B)
    HH = NH // 2
    with ExitStack() as ctx:
        def sb(name, shape, dt=F32):
            return ctx.enter_context(nc.sbuf_tensor(name, shape, dt))

        xn = sb("xn", [T, 2, 128])
        xT = sb("xT", [DH, 2, T])
        t1 = sb("t1", [T, QK + DH])
        t2 = sb("t2", [T, QK + DH])
        qr = sb("qr", [T, QK + DH])
        sqb = sb("sqb", [T, QK + DH])
        ssq = sb("ssq", [T, NH + 1])
        lrq = sb("lrq", [T, NH + 1])
        rq = sb("rq", [T, 2, NH + 1])
        qT = sb("qT", [128, 2, HH, T])
        kn = sb("kn", [T, 2, DH])
        kT = sb("kT", [128, 2, T])
        vt = sb("vt", [T, 2, DH])
        vs = sb("vs", [T, 2, DH])
        mx = sb("mx", [T, 2, HH])
        nb = sb("nb", [T, 2, HH])
        pb = sb("pb", [T, 2, NH, T])
        sm = sb("sm", [T, 2, NH])
        rc = sb("rc", [T, 2, NH])
        pT = sb("pT", [T, NH, T])
        oT = sb("oT", [128, HH, T])
        st = sb("ast", [T, 6])
        mvs = sb("amvs", [T, 2])
        lrs = sb("alrs", [T, B])

        filled = {s: sem("af_" + s) for s, _, _ in ORDER_ATT}
        names = ("xn", "xT", "tq0", "tq1", "tk", "v", "qr0", "qr1", "qrk", "sqa", "sqb", "ssq", "lrq", "rq", "qT0",
                 "qT1", "kn", "kT", "vs", "mx0", "mx1", "nb0", "nb1", "ex0", "ex1", "rc0", "rc1", "pn0", "pn1",
                 "pT0", "pT1", "pT2", "pT3", "oT0", "oT1", "res", "st", "mv", "all", "zero")
        S = {n: sem("a_" + n) for n in names}
        read = {"q0": S["tq0"], "q1": S["tq1"], "kv": S["v"], "sc0": S["ex0"], "sc1": S["ex1"], "qt0": S["qT0"],
                "qt1": S["qT1"], "kt": S["kT"], "pt0": S["pT0"], "pt1": S["pT1"], "pt2": S["pT2"], "pt3": S["pT3"],
                "pv0": S["oT0"], "pv1": S["oT1"], "wo": S["res"], "xt": S["xT"]}
        M0, M1 = 6, 7
        sc = [ps[:, 2 * h:2 * h + 2, :].rearrange("p a b -> p (a b)").rearrange("p (h s) -> p h s", h=HH)
              for h in range(2)]

        with nc.Block() as block:
            @block.tensor
            def _(pe):
                def bank_free(stage, i, lo):
                    p = prev(stage, i, lo)
                    if p:
                        pe.wait_ge(read[p[0]], p[1] + 1)

                def x_t(i, lo):
                    bank_free("xt", i, lo)
                    pe.wait_ge(S["xn"], i + 1)
                    pe.transpose(ps[:, M1, 0:T], xn[:, lo % 2, :], K["ident"]).then_inc(filled["xt"], 1)

                def project(stage, bank, at, n):
                    def f(i, lo):
                        bank_free(stage, i, lo)
                        pe.wait_ge(S["xT"], i + 1)
                        pe.matmul(ps[:, bank, 0:n], xT[:, lo % 2, :], wqkv[:, at:at + n], start=True,
                                  stop=True).then_inc(filled[stage], 1)
                    return f

                def q_t(h, bank):
                    def f(i, lo):
                        bank_free(f"qt{h}", i, lo)
                        pe.wait_ge(S[f"qr{h}"], i + 1)
                        for p in range(4):
                            at = (4 * h + p) * 2 * DH
                            last = pe.transpose(ps[:, bank, p * T:(p + 1) * T], qr[:, at:at + 2 * DH], K["ident"])
                        last.then_inc(filled[f"qt{h}"], 1)
                    return f

                def k_t(i, lo):
                    bank_free("kt", i, lo)
                    pe.wait_ge(S["kn"], i + 1)
                    pe.transpose(ps[:, M0, 0:T], kn[:].rearrange("p a d -> p (a d)"), K["ident"]
                                 ).then_inc(filled["kt"], 1)

                def scores(h):
                    def f(i, lo):
                        bank_free(f"sc{h}", i, lo)
                        if h == 0:
                            pe.wait_ge(S["kT"], i + 1)
                        pe.wait_ge(S[f"qT{h}"], i + 1)
                        for j in range(2):
                            pe.matmul(ps[:, 2 * h + j, :], identb[:], maskb[:].rearrange("p a s -> p (a s)"),
                                      start=True, stop=False, skip_group_check=True)
                        for n in range(4):
                            for j in range(2):
                                o = 64 * j
                                last = pe.matmul(ps[:, 2 * h + j, n * T:(n + 1) * T],
                                                 qT[o:o + 64, lo % 2, 4 * h + n, :], kT[o:o + 64, lo % 2, :],
                                                 start=False, stop=(n == 3), skip_group_check=True)
                        last.then_inc(filled[f"sc{h}"], 1)
                    return f

                def p_t(j):
                    def f(i, lo):
                        bank_free(f"pt{j}", i, lo)
                        if j % 2 == 0:
                            pe.wait_ge(S[f"pn{j // 2}"], i + 1)
                        for n in range(4):
                            last = pe.transpose(ps[:, 4 + j % 2, n * T:(n + 1) * T], pb[:, lo % 2, 4 * j + n, :],
                                                K["ident"])
                        last.then_inc(filled[f"pt{j}"], 1)
                    return f

                def p_v(h):
                    def f(i, lo):
                        bank_free(f"pv{h}", i, lo)
                        if h == 0:
                            pe.wait_ge(S["vs"], i + 1)
                        pe.wait_ge(S[f"pT{2 * h}"], i + 1)
                        pe.wait_ge(S[f"pT{2 * h + 1}"], i + 1)
                        for odd in range(2):
                            last = pe.matmul(ps[64 * odd:64 * odd + 64, M1, :], vs[:, lo % 2, :],
                                             pT[:, 8 * h + odd:8 * h + 8:2, :], start=True, stop=True)
                        last.then_inc(filled[f"pv{h}"], 1)
                    return f

                def w_o(i, lo):
                    bank_free("wo", i, lo)
                    pe.wait_ge(S["oT0"], i + 1)
                    pe.wait_ge(S["oT1"], i + 1)
                    for p in range(HH):
                        last = pe.matmul(ps[:, M0, 0:DH], oT[:, p, :], wo[:, p, :], start=(p == 0),
                                         stop=(p == HH - 1))
                    last.then_inc(filled["wo"], 1)

                stages = {"q0": project("q0", M0, 0, 512), "sc0": scores(0), "q1": project("q1", M1, 512, 512),
                          "pt0": p_t(0), "pt1": p_t(1), "kv": project("kv", M0, QK, 2 * DH), "pv0": p_v(0),
                          "sc1": scores(1), "qt0": q_t(0, M0), "pt2": p_t(2), "pt3": p_t(3), "qt1": q_t(1, M1),
                          "kt": k_t, "pv1": p_v(1), "wo": w_o, "xt": x_t}
                pipeline(pe, B, [(stages[s], lag) for s, lag, _ in ORDER_ATT])

            @block.vector
            def _(ve):
                def layer_norm(i, lo):
                    if lo >= 2:
                        ve.wait_ge(filled["xt"], i - 1)
                    ve.tensor_scalar(xn[:, lo % 2, 0:DH], h4[:, bass.ds(i, 1), :].rearrange("p a n -> p (a n)"),
                                     mv[:, bass.ds(i, 1), 0:1].rearrange("p a n -> p (a n)"),
                                     rstd[:, bass.ds(i, 1)], ALU.subtract, ALU.mult).then_inc(S["xn"], 1)

                def x_copy(i, lo):
                    ve.wait_ge(filled["xt"], i + 1)
                    if lo >= 2:
                        ve.wait_ge(filled["kv"], i - 1)
                    ve.tensor_copy(xT[:, lo % 2, :], ps[0:DH, M1, 0:T]).then_inc(S["xT"], 1)

                def rope(stage, bank, n, at, products, added):
                    def f(i, lo):
                        ve.wait_ge(filled[stage], i + 1)
                        if lo >= 1:
                            ve.wait_ge(S[added], i)
                        x = ps[:, bank, 0:n * DH].rearrange("p (h d) -> p h d", h=n)
                        a = t1[:, at:at + n * DH].rearrange("p (h d) -> p h d", h=n)
                        b = t2[:, at:at + n * DH].rearrange("p (h d) -> p h d", h=n)
                        half = DH // 2
                        cos = K["ropec"].unsqueeze(1).to_broadcast([T, n, DH])
                        sin = K["ropes"].unsqueeze(1).to_broadcast([T, n, DH])
                        ve.tensor_tensor(a, x, cos, ALU.mult)
                        ve.tensor_tensor(b[:, :, 0:half], x[:, :, half:DH], sin[:, :, 0:half], ALU.mult)
                        ve.tensor_tensor(b[:, :, half:DH], x[:, :, 0:half], sin[:, :, half:DH], ALU.mult
                                         ).then_inc(S[products], 1)
                    return f

                def v_copy(i, lo):
                    if lo >= 2:
                        ve.wait_ge(S["vs"], i - 1)
                    ve.tensor_copy(vt[:, lo % 2, :], ps[:, M0, DH:2 * DH]).then_inc(S["v"], 1)

                def sums(i, lo):
                    ve.wait_ge(S["sqa"], i + 1)
                    ve.wait_ge(S["sqb"], i + 1)
                    if lo >= 1:
                        ve.wait_ge(S["lrq"], i)
                    ve.tensor_reduce(ssq[:], sqb[:].rearrange("p (h d) -> p h d", h=NH + 1), AX_X, ALU.add
                                     ).then_inc(S["ssq"], 1)

                def k_norm(i, lo):
                    ve.wait_ge(S["rq"], i + 1)
                    if lo >= 1:
                        ve.wait_ge(filled["kt"], i)
                    ve.scalar_tensor_tensor(out=kn[:], in0=qr[:, QK:QK + DH].unsqueeze(1).to_broadcast([T, 2, DH]),
                                            scalar=rq[:, lo % 2, NH:NH + 1],
                                            in1=wqk[:].unsqueeze(1).to_broadcast([T, 2, DH]), op0=ALU.mult,
                                            op1=ALU.mult).then_inc(S["kn"], 1)

                def k_copy(i, lo):
                    ve.wait_ge(filled["kt"], i + 1)
                    if lo >= 2:
                        ve.wait_ge(filled["sc1"], i - 1)
                    ve.tensor_copy(kT[:, lo % 2, :], ps[:, M0, 0:T]).then_inc(S["kT"], 1)

                def maximum(h):
                    def f(i, lo):
                        ve.wait_ge(filled[f"sc{h}"], i + 1)
                        if lo >= 1:
                            ve.wait_ge(S[f"nb{h}"], i)
                        ve.tensor_reduce(mx[:, h, :], sc[h], AX_X, ALU.max).then_inc(S[f"mx{h}"], 1)
                        ve.wait_ge(S[f"mx{h}"], i + 1)
                        if lo >= 1:
                            ve.wait_ge(S[f"ex{h}"], i)
                        ve.scalar_tensor_tensor(out=nb[:, h, :].rearrange("p (j n) -> p j n", j=2),
                                                in0=mx[:, h, :].rearrange("p (j n) -> p j n", j=2), scalar=-1.0,
                                                in1=rq[:, lo % 2, h * HH:(h + 1) * HH].rearrange(
                                                    "p (n j) -> p j n", j=2), op0=ALU.mult,
                                                op1=ALU.mult).then_inc(S[f"nb{h}"], 1)
                    return f

                def recip(h):
                    def f(i, lo):
                        ve.wait_ge(S[f"ex{h}"], i + 1)
                        if lo >= 2:
                            ve.wait_ge(S[f"pn{h}"], i - 1)
                        ve.reciprocal(rc[:, lo % 2, h * HH:(h + 1) * HH], sm[:, lo % 2, h * HH:(h + 1) * HH]
                                      ).then_inc(S[f"rc{h}"], 1)
                    return f

                def p_copy(j):
                    def f(i, lo):
                        ve.wait_ge(filled[f"pt{j}"], i + 1)
                        if lo >= 1:
                            ve.wait_ge(filled[f"pv{j // 2}"], i)
                        ve.tensor_copy(pT[:, 4 * j:4 * j + 4, :],
                                       ps[:, 4 + j % 2, :].rearrange("p (h t) -> p h t", h=4)).then_inc(S[f"pT{j}"], 1)
                    return f

                def residual(i, lo):
                    ve.wait_ge(filled["wo"], i + 1)
                    h = h4[:, bass.ds(i, 1), :].rearrange("p a n -> p (a n)")
                    ve.tensor_tensor(h, ps[:, M0, 0:DH], h, ALU.add).then_inc(S["res"], 1)
                    ve.wait_ge(S["res"], i + 1)
                    stand_alone(ve, V)
                    ve.bn_stats(st[:], h).then_inc(S["st"], 1)
                    ve.wait_ge(S["st"], 2 * i + 1)
                    if lo >= 1:
                        ve.wait_ge(S["mv"], i)
                    stand_alone(ve, V)
                    ve.bn_aggr(mvs[:], st[:]).then_inc(S["st"], 1)
                    ve.wait_ge(S["st"], 2 * i + 2)
                    ve.tensor_copy(mv[:, bass.ds(i, 1), :].rearrange("p a n -> p (a n)"), mvs[:]).then_inc(S["mv"], 1)

                ve.memset(xn[:], 0.0).then_inc(S["zero"], 1)
                ve.wait_ge(S["zero"], 1)
                pipeline(ve, B, [(recip(1), 3), (rope("q0", M0, 8, 0, "tq0", "qr0"), 1), (maximum(0), 2),
                                 (rope("q1", M1, 8, 512, "tq1", "qr1"), 1), (p_copy(0), 3), (p_copy(1), 3),
                                 (rope("kv", M0, 1, QK, "tk", "qrk"), 1), (v_copy, 1), (maximum(1), 2),
                                 (layer_norm, 0), (sums, 1), (p_copy(2), 3), (p_copy(3), 3), (k_norm, 1),
                                 (recip(0), 2), (k_copy, 1), (residual, 3), (x_copy, 0)])
                ve.wait_ge(S["all"], 1)

            @block.scalar
            def _(ac):
                ac.preload_act_table_set("natural_log_exp_and_others")

                def square0(i, lo):
                    ac.wait_ge(S["qr0"], i + 1)
                    if lo >= 1:
                        ac.wait_ge(S["ssq"], i)
                    ac.activation(sqb[:, 0:512], qr[:, 0:512], ACT.Square).then_inc(S["sqa"], 1)

                def square1(i, lo):
                    ac.wait_ge(S["qr1"], i + 1)
                    ac.wait_ge(S["qrk"], i + 1)
                    ac.activation(sqb[:, 512:QK + DH], qr[:, 512:QK + DH], ACT.Square).then_inc(S["sqb"], 1)

                def rms(i, lo):
                    ac.wait_ge(S["ssq"], i + 1)
                    ac.activation(lrq[:], ssq[:], ACT.Ln, bias=epsc[:, 1:2], scale=1.0 / DH).then_inc(S["lrq"], 1)
                    ac.wait_ge(S["lrq"], i + 1)
                    if lo >= 2:
                        ac.wait_ge(S["nb1"], i - 1)
                    ac.activation(rq[:, lo % 2, :], lrq[:], ACT.Exp, scale=-0.5).then_inc(S["rq"], 1)

                def exps(h):
                    def f(i, lo):
                        ac.wait_ge(S[f"nb{h}"], i + 1)
                        if lo >= 2:
                            ac.wait_ge(filled[f"pt{2 * h + 1}"], i - 1)
                            ac.wait_ge(S[f"rc{h}"], i - 1)
                        for n in range(HH):
                            head = h * HH + 2 * (n % 4) + n // 4
                            last = ac.activation(pb[:, lo % 2, head, :], sc[h][:, n, :], ACT.Exp,
                                                 bias=nb[:, h, n:n + 1], scale=rq[:, lo % 2, head:head + 1],
                                                 accum_out=sm[:, lo % 2, head:head + 1])
                        last.then_inc(S[f"ex{h}"], 1)
                    return f

                def q_copy(h, bank):
                    def f(i, lo):
                        ac.wait_ge(filled[f"qt{h}"], i + 1)
                        if lo >= 2:
                            ac.wait_ge(filled[f"sc{h}"], i - 1)
                        ac.activation(qT[:, lo % 2, 4 * h:4 * h + 4, :],
                                      ps[:, bank, :].rearrange("p (h t) -> p h t", h=4), ACT.Copy
                                      ).then_inc(S[f"qT{h}"], 1)
                    return f

                def o_copy(h):
                    def f(i, lo):
                        ac.wait_ge(filled[f"pv{h}"], i + 1)
                        if lo >= 1:
                            ac.wait_ge(filled["wo"], i)
                        ac.activation(oT[:, 4 * h:4 * h + 4, :], ps[:, M1, :].rearrange("p (h t) -> p h t", h=4),
                                      ACT.Copy).then_inc(S[f"oT{h}"], 1)
                    return f

                pipeline(ac, B, [(square0, 1), (exps(0), 2), (square1, 1), (o_copy(0), 3), (rms, 1), (q_copy(0, M0), 1),
                                 (q_copy(1, M1), 1), (o_copy(1), 3), (exps(1), 2)])
                ac.wait_ge(S["mv"], B)
                ac.activation(lrs[:], mv[:, :, 1], ACT.Ln, bias=epsc[:, 0:1]).then_inc(S["all"], 1)
                ac.wait_ge(S["all"], 1)
                ac.activation(rstd[:], lrs[:], ACT.Exp, scale=-0.5).then_inc(S["all"], 1)
                ac.wait_ge(S["all"], 2)

            @block.gpsimd
            def _(po):
                def rotate(part, at, n, products):
                    def f(i, lo):
                        po.wait_ge(S[products], i + 1)
                        if lo >= 1:
                            if part == "k":
                                po.wait_ge(S["kn"], i)
                            else:
                                po.wait_ge(filled[f"qt{part}"], i)
                            po.wait_ge(S["sqa" if part == "0" else "sqb"], i)
                        po.tensor_tensor(qr[:, at:at + n], t1[:, at:at + n], t2[:, at:at + n], ALU.add
                                         ).then_inc(S["qr" + part], 1)
                    return f

                def normalize(h):
                    def f(i, lo):
                        po.wait_ge(S[f"rc{h}"], i + 1)
                        p = pb[:, lo % 2, h * HH:(h + 1) * HH, :]
                        po.tensor_tensor(p, p, rc[:, lo % 2, h * HH:(h + 1) * HH].unsqueeze(2).to_broadcast([T, HH, T]),
                                         ALU.mult).then_inc(S[f"pn{h}"], 1)
                    return f

                def v_pass(i, lo):
                    po.wait_ge(S["v"], i + 1)
                    if lo >= 2:
                        po.wait_ge(filled["pv1"], i - 1)
                    po.tensor_tensor(vs[:, lo % 2, :], vt[:, lo % 2, :], K["ones"][:, 0:DH], ALU.mult
                                     ).then_inc(S["vs"], 1)

                pipeline(po, B, [(rotate("0", 0, 512, "tq0"), 1), (normalize(1), 3), (rotate("1", 512, 512, "tq1"), 1),
                                 (rotate("k", QK, DH, "tk"), 1), (v_pass, 2), (normalize(0), 2)])


def ffn_phase(nc, V, out, sem):
    ps, K, epsc = V["ps"], V["K"], V["epsc"]
    h4, mv, rstd = V["h4"], V["mv"], V["rstd"]
    fcol, fwr, fbr, fw1, fb1, fw2, fb2 = (V[n] for n in ("fcol", "fwr", "fbr", "fw1", "fb1", "fw2", "fb2"))
    T, NT = C, 4 * C
    with ExitStack() as ctx:
        def sb(name, shape, dt=F32):
            return ctx.enter_context(nc.sbuf_tensor(name, shape, dt))

        xa = sb("xa", [DH, B * T])
        wf = sb("wf", [T, B, E])
        xs1 = sb("xs1", [T, 2, 4, DH])
        st = sb("fst", [T, 4, 6])
        m3 = sb("fm3", [T, 2, 4, 2])
        l3 = sb("fl3", [T, 4])
        r3 = sb("fr3", [T, 2, 4])
        xs2 = sb("xs2", [T, 2, 4, 128])
        xt = sb("fxt", [DH, 2, NT])
        lg = sb("flg", [T, 4, E])
        top = sb("ftop", [T, 4, 8])
        idx = sb("fidx", [T, 4, 8], U32)
        idf = sb("fidf", [T, 4, 2])
        df = sb("fdf", [T, 4])
        ex = sb("fex", [T, 4])
        ex1 = sb("fex1", [T, 4])
        w12 = sb("fw12", [T, 2, 4])
        hot = sb("fhot", [T, 2, 4, E])
        filled = {s: sem("rf_" + s) for s, _, _ in ORDER_ROUTE}
        names = ("x1", "st", "m3", "l3", "r3", "x2", "xt", "xa", "lg", "top", "idx", "df", "ex", "w", "wf", "done", "zero")
        S = {n: sem("r_" + n) for n in names}
        prev = previous(ORDER_ROUTE, QUADS)
        read = {"xt": S["xt"], "lg": S["lg"]}

        with nc.Block() as block:
            @block.tensor
            def _(pe):
                def x_t(i, lo):
                    p = prev("xt", i, lo)
                    if p:
                        pe.wait_ge(read[p[0]], p[1] + 1)
                    pe.wait_ge(S["x2"], i + 1)
                    for r in range(4):
                        last = pe.transpose(ps[:, 0, r * T:(r + 1) * T], xs2[:, lo % 2, r, :], K["ident"])
                    last.then_inc(filled["xt"], 1)

                def route(i, lo):
                    p = prev("lg", i, lo)
                    if p:
                        pe.wait_ge(read[p[0]], p[1] + 1)
                    pe.wait_ge(S["xt"], i + 1)
                    for r in range(4):
                        last = pe.matmul(ps[:, 1, r * E:(r + 1) * E], xt[:, lo % 2, r * T:(r + 1) * T], fwr[:],
                                         start=True, stop=True)
                    last.then_inc(filled["lg"], 1)

                pipeline(pe, QUADS, [(x_t, 1), (route, 2)])

            @block.scalar
            def _(ac):
                ac.preload_act_table_set("natural_log_exp_and_others")

                def rsqrt(i, lo):
                    ac.wait_ge(S["m3"], i + 1)
                    ac.activation(l3[:], m3[:, lo % 2, :, 1], ACT.Ln, bias=epsc[:, 0:1]).then_inc(S["l3"], 1)
                    ac.wait_ge(S["l3"], i + 1)
                    if lo >= 2:
                        ac.wait_ge(S["x2"], i - 1)
                    ac.activation(r3[:, lo % 2, :], l3[:], ACT.Exp, scale=-0.5).then_inc(S["r3"], 1)

                def affine(i, lo):
                    ac.wait_ge(filled["xt"], i + 1)
                    if lo >= 2:
                        ac.wait_ge(filled["lg"], i - 1)
                        ac.wait_ge(S["xa"], i - 1)
                    ac.activation(xt[:, lo % 2, :], ps[0:DH, 0, :], ACT.Identity, bias=fcol[:, 1:2],
                                  scale=fcol[:, 0:1]).then_inc(S["xt"], 1)

                def expd(i, lo):
                    ac.wait_ge(S["df"], i + 1)
                    if lo >= 1:
                        ac.wait_ge(S["w"], 3 * i)
                    ac.activation(ex[:], df[:], ACT.Exp).then_inc(S["ex"], 1)

                pipeline(ac, QUADS, [(rsqrt, 0), (affine, 1), (expd, 2)])

            @block.gpsimd
            def _(po):
                def keep(i, lo):
                    po.wait_ge(S["xt"], i + 1)
                    po.tensor_copy(xa[:, bass.ds(i * NT, NT)], xt[:, lo % 2, :]).then_inc(S["xa"], 1)

                pipeline(po, QUADS, [(keep, 1)])

            @block.vector
            def _(ve):
                def first_norm(i, lo):
                    if lo >= 2:
                        ve.wait_ge(S["x2"], i - 1)
                    for r in range(4):
                        last = ve.tensor_scalar(xs1[:, lo % 2, r, :],
                                                h4[:, bass.ds(4 * i + r, 1), :].rearrange("p a n -> p (a n)"),
                                                mv[:, bass.ds(4 * i + r, 1), 0:1].rearrange("p a n -> p (a n)"),
                                                rstd[:, bass.ds(4 * i + r, 1)], ALU.subtract, ALU.mult)
                    last.then_inc(S["x1"], 1)
                    ve.wait_ge(S["x1"], i + 1)
                    if lo >= 1:
                        ve.wait_ge(S["m3"], i)
                    for r in range(4):
                        last = ve.bn_stats(st[:, r, :], xs1[:, lo % 2, r, :])
                    last.then_inc(S["st"], 1)
                    ve.wait_ge(S["st"], i + 1)
                    if lo >= 2:
                        ve.wait_ge(S["r3"], i - 1)
                    stand_alone(ve, V)
                    for r in range(4):
                        last = ve.bn_aggr(m3[:, lo % 2, r, :], st[:, r, :])
                    last.then_inc(S["m3"], 1)

                def second_norm(i, lo):
                    ve.wait_ge(S["r3"], i + 1)
                    if lo >= 2:
                        ve.wait_ge(filled["xt"], i - 1)
                    for r in range(4):
                        last = ve.tensor_scalar(xs2[:, lo % 2, r, 0:DH], xs1[:, lo % 2, r, :], m3[:, lo % 2, r, 0:1],
                                                r3[:, lo % 2, r:r + 1], ALU.subtract, ALU.mult)
                    last.then_inc(S["x2"], 1)

                def best_two(i, lo):
                    ve.wait_ge(filled["lg"], i + 1)
                    if lo >= 1:
                        ve.wait_ge(S["idx"], 2 * i)
                    ve.tensor_tensor(lg[:], ps[:, 1, 0:4 * E].rearrange("p (r e) -> p r e", r=4),
                                     fbr[:].unsqueeze(1).to_broadcast([T, 4, E]), ALU.add).then_inc(S["lg"], 1)
                    ve.wait_ge(S["lg"], i + 1)
                    stand_alone(ve, V)
                    for r in range(4):
                        last = ve.max(top[:, r, :], lg[:, r, :])
                    last.then_inc(S["top"], 1)
                    ve.wait_ge(S["top"], i + 1)
                    if lo >= 1:
                        ve.wait_ge(S["ex"], i)
                    ve.tensor_tensor(df[:], top[:, :, 1], top[:, :, 0], ALU.subtract).then_inc(S["df"], 1)
                    for r in range(4):
                        last = ve.max_index(idx[:, r, :], top[:, r, :], lg[:, r, :])
                    last.then_inc(S["idx"], 1)
                    ve.wait_ge(S["idx"], 2 * i + 1)
                    ve.tensor_copy(idf[:], idx[:, :, 0:2]).then_inc(S["idx"], 1)

                def spread(i, lo):
                    ve.wait_ge(S["ex"], i + 1)
                    ve.wait_ge(S["idx"], 2 * i + 2)
                    if lo >= 1:
                        ve.wait_ge(S["wf"], 2 * i)
                    ve.tensor_scalar(ex1[:], ex[:], 1.0, None, ALU.add).then_inc(S["w"], 1)
                    ve.wait_ge(S["w"], 3 * i + 1)
                    ve.reciprocal(w12[:, 0, :], ex1[:]).then_inc(S["w"], 1)
                    ve.wait_ge(S["w"], 3 * i + 2)
                    ve.tensor_tensor(w12[:, 1, :], w12[:, 0, :], ex[:], ALU.mult).then_inc(S["w"], 1)
                    ve.wait_ge(S["w"], 3 * i + 3)
                    for k in range(2):
                        last = ve.tensor_tensor(hot[:, k, :, :], K["iota8"].unsqueeze(1).to_broadcast([T, 4, E]),
                                                idf[:, :, k:k + 1].to_broadcast([T, 4, E]), ALU.is_equal)
                    last.then_inc(S["wf"], 1)
                    ve.wait_ge(S["wf"], 2 * i + 1)
                    ve.tensor_tensor(hot[:], hot[:], w12[:].unsqueeze(3).to_broadcast([T, 2, 4, E]), ALU.mult
                                     ).then_inc(S["done"], 1)
                    ve.wait_ge(S["done"], i + 1)
                    ve.tensor_tensor(wf[:, bass.ds(4 * i, 4), :], hot[:, 0, :, :], hot[:, 1, :, :], ALU.add
                                     ).then_inc(S["wf"], 1)

                ve.memset(xs2[:], 0.0).then_inc(S["zero"], 1)
                ve.wait_ge(S["zero"], 1)
                pipeline(ve, QUADS, [(first_norm, 0), (second_norm, 0), (best_two, 2), (spread, 2)])
                ve.wait_ge(S["wf"], 2 * QUADS)

        hh = sb("fhh", [HID, 2, 2 * T])
        yb = sb("fyb", [T, 2, 2, E * DH])
        yw = sb("fyw", [T, 2, 2, E * DH])
        ys = sb("fys", [T, 2, DH])
        yo = sb("fyo", [T, 2, 2, DH])
        filled = {s: sem("ef_" + s) for s, _, _ in ORDER_EXP}
        X = {n: sem("e_" + n) for n in ("yb", "yw", "ys", "yo")}
        s_h = [sem(f"e_h{e}") for e in range(E)]
        stored = [sem("stored0"), sem("stored1")]
        out_v = out.rearrange("b t d -> t b d")

        with nc.Block() as block:
            @block.tensor
            def _(pe):
                def up(e):
                    def f(i, lo):
                        pe.matmul(ps[:, e % 2, 0:2 * T], fw1[:, e, :], xa[:, bass.ds(i * 2 * T, 2 * T)], start=True,
                                  stop=True).then_inc(filled[f"w1{e}"], 1)
                    return f

                def down(e):
                    def f(i, lo):
                        pe.wait_ge(s_h[e], i + 1)
                        if e == 0 and lo >= 2:
                            pe.wait_ge(X["yb"], i - 1)
                        for r in range(2):
                            last = pe.matmul(ps[:, 2 + 2 * (lo % 2) + r, e * DH:(e + 1) * DH],
                                             hh[:, e % 2, r * T:(r + 1) * T], fw2[:, e, :], start=True, stop=True,
                                             skip_group_check=True)
                        last.then_inc(filled[f"w2{e}"], 1)
                    return f

                stages = {**{f"w1{e}": up(e) for e in range(E)}, **{f"w2{e}": down(e) for e in range(E)}}
                pipeline(pe, PAIRS, [(stages[s], lag) for s, lag, _ in ORDER_EXP])

            @block.scalar
            def _(ac):
                def gelu(e):
                    def f(i, lo):
                        ac.wait_ge(filled[f"w1{e}"], i + 1)
                        if e >= 2:
                            ac.wait_ge(filled[f"w2{e - 2}"], i + 1)
                        elif lo >= 1:
                            ac.wait_ge(filled[f"w2{e + E - 2}"], i)
                        ac.activation(hh[:, e % 2, :], ps[:, e % 2, 0:2 * T], ACT.Gelu,
                                      bias=fb1[:, e:e + 1]).then_inc(s_h[e], 1)
                    return f

                ac.preload_act_table_set("gelu_and_others")
                pipeline(ac, PAIRS, [(gelu(e), 0) for e in range(E)])

            @block.vector
            def _(ve):
                def bias(i, lo):
                    ve.wait_ge(filled["w27"], i + 1)
                    if lo >= 2:
                        ve.wait_ge(X["yw"], i - 1)
                    ve.tensor_tensor(yb[:, lo % 2, :, :], ps[:, 2 + 2 * (lo % 2):4 + 2 * (lo % 2), :],
                                     fb2[:].unsqueeze(1).to_broadcast([T, 2, E * DH]), ALU.add).then_inc(X["yb"], 1)

                def combine(i, lo):
                    ve.wait_ge(X["yw"], i + 1)
                    if lo >= 1:
                        ve.wait_ge(X["yo"], i)
                    ve.tensor_reduce(ys[:], yw[:, lo % 2, :, :].rearrange("p r (e d) -> p r d e", e=E), AX_X, ALU.add
                                     ).then_inc(X["ys"], 1)
                    ve.wait_ge(X["ys"], i + 1)
                    if lo >= 2:
                        ve.wait_ge(stored[lo % 2], i * 8 - 8 * (lo % 2))
                    ve.tensor_tensor(yo[:, lo % 2, :, :], ys[:], h4[:, bass.ds(2 * i, 2), :], ALU.add
                                     ).then_inc(X["yo"], 1)

                pipeline(ve, PAIRS, [(bias, 1), (combine, 2)])

            @block.gpsimd
            def _(po):
                def weigh(i, lo):
                    po.wait_ge(X["yb"], i + 1)
                    if lo >= 2:
                        po.wait_ge(X["ys"], i - 1)
                    for r in range(2):
                        last = po.tensor_tensor(yw[:, lo % 2, r, :].rearrange("p (e d) -> p e d", e=E),
                                                yb[:, lo % 2, r, :].rearrange("p (e d) -> p e d", e=E),
                                                wf[:, bass.ds(2 * i + r, 1), :].rearrange("p a e -> p (a e)")
                                                .unsqueeze(2).to_broadcast([T, E, DH]), ALU.mult)
                    last.then_inc(X["yw"], 1)

                pipeline(po, PAIRS, [(weigh, 1)])

            @block.sync
            def _(sp):
                def store(i, lo):
                    sp.wait_ge(X["yo"], i + 1)
                    sp.dma_start(out_v[:, bass.ds(2 * i, 2), :], yo[:, lo % 2, :, :]).then_inc(stored[lo % 2], 16)

                pipeline(sp, PAIRS, [(store, 0)])
                for s in stored:
                    sp.wait_ge(s, 16 * (PAIRS // 2))


def shape_constants():
    i, j = np.arange(128)[:, None], np.arange(128)[None, :]
    same = (i // KR == j // KR) & (i < GR) & (j < GR)
    freqs = (np.float32(10000.0) ** (np.float32(-2.0) * np.arange(DH // 2, dtype=np.float32) / np.float32(DH)))
    theta = np.arange(128, dtype=np.float32)[:, None] * freqs.astype(np.float32)[None, :]
    cos, sin = np.cos(theta), np.sin(theta)
    cap = np.ones((128, TN))
    cap[:, TN - 1] = 3e38
    cols = {"ident": i == j, "cmat": (i == j) - 1.0 / C, "ones127": np.full((128, 128), 1.0 / (C - 1)),
            "gmask": same / (C - 1.0), "blkones": same, "tri": i <= j, "stri": i < j,
            "ones": np.ones((128, 128)), "mask": np.where(j <= i, 0.0, -1e30),
            "iota": np.broadcast_to(np.arange(TN), (128, TN)), "cap": cap,
            "ropec": np.concatenate([cos, cos], 1), "ropes": np.concatenate([-sin, sin], 1),
            "iota8": np.broadcast_to(np.arange(E), (128, E))}
    return np.concatenate([np.asarray(cols[n], np.float32) for n, _ in CONSTS], 1)


def patch_index():
    g, k, c = np.arange(NG)[:, None, None], np.arange(K0)[None, :, None], np.arange(GC)[None, None, :]
    q, m = g // 2, (g % 2) * GC + c
    n = 4 * (m + (q < 2)) + q - 2
    s = ST0 * n + k - PAD0
    s = np.abs(s)
    return np.where(s >= L, 2 * (L - 1) - s, s)


def kernel(**inputs):
    import concourse.bacc as _bacc
    from concourse.bass_utils import run_bass_kernel_spmd as _run

    a = {n.replace("L0_", ""): np.asarray(v) for n, v in inputs.items()}
    x = a["x"].reshape(B, L)
    x8 = np.ones((PAIRS, NG, KR, 2, GC), np.float32)
    x8[:, :, 0:K0] = x[:, patch_index()].reshape(PAIRS, 2, NG, K0, GC).transpose(0, 2, 3, 1, 4)
    f0 = np.concatenate([a["tok_conv0_w"].reshape(C, K0).T, a["tok_conv0_b"].reshape(1, C)], 0)
    w0 = np.zeros((NG, KR, NG + 1, C), np.float32)
    for g in range(NG):
        w0[g, :, g] = f0
        w0[g, :, NG] = f0
    taps = [a[f"tok_conv{n}_w"].transpose(1, 2, 0) for n in (1, 2, 3)]
    par = np.stack([a[f"tok_conv{n}_b"] for n in (1, 2, 3)] + [a[f"tok_n{n}_w"] for n in range(5)]
                   + [a[f"tok_n{n}_b"] for n in range(5)], 1)
    mcol = np.concatenate([a["tok_mlp_b1"].reshape(4, 128).T, a["tok_mlp_b2"].reshape(4, 128).T,
                           a["tok_mlp_w3"].reshape(4, 128).T,
                           np.broadcast_to(a["tok_mlp_b3"].reshape(1, 1), (128, 1))], 1)
    halves = np.concatenate([np.arange(0, DH, 2), np.arange(1, DH, 2)])
    wq = a["attn_wq"].reshape(NH, DH, DH)[:, halves].reshape(NH * DH, DH)
    wkv = a["attn_wkv"]
    arrays = {
        "x8": x8.reshape(PAIRS * GR, 2 * GC),
        "const": shape_constants(),
        "par": par,
        "w0": w0.reshape(GR, NG + 1, C),
        "w123": np.concatenate(taps, 1),
        "mw1": a["tok_mlp_w1"],
        "mw2": a["tok_mlp_w2"].reshape(4, 128, DMLP).transpose(1, 0, 2),
        "mcol": mcol,
        "wqkv": np.concatenate([wq.T, wkv[0:DH][halves].T, wkv[DH:].T], 1),
        "wo": a["attn_wo"].T.reshape(NH // 2, 2 * DH, DH).transpose(1, 0, 2),
        "qkw": np.broadcast_to(np.concatenate([a["attn_q_norm_w"][halves], a["attn_k_norm_w"][halves]]), (128, 2 * DH)),
        "fcol": np.stack([a["ffn_gamma"], a["ffn_beta"]], 1),
        "fwr": a["ffn_Wr"],
        "fbr": np.broadcast_to(a["ffn_br"], (128, E)),
        "fw1": a["ffn_W1"].transpose(1, 0, 2),
        "fb1": a["ffn_b1"].T,
        "fw2": a["ffn_W2"].transpose(1, 0, 2),
        "fb2": np.broadcast_to(a["ffn_b2"].reshape(E * DH), (128, E * DH)),
    }
    nc = _bacc.Bacc("TRN2", target_bir_lowering=False, num_devices=1)
    A = {}
    for name in list(arrays):
        v = np.ascontiguousarray(arrays.pop(name))
        arrays[f"in_{name}"] = v
        A[name] = nc.dram_tensor(f"in_{name}", v.shape, F32, kind="ExternalInput").ap()
    out = nc.dram_tensor("out", (B, C, TN), F32, kind="ExternalOutput").ap()
    audio_tower(nc, A, out)
    r = _run(nc, [arrays], core_ids=[0])
    return r.results[0]["out"]
```
